# Optimizing a Trainium2 kernel written in Bass

```python
import numpy as np
import jax
import jax.numpy as jnp

def _softmax(x, axis=-1):
    return jax.nn.softmax(x, axis=axis)

def _gelu(x):
    return jax.nn.gelu(x, approximate=True)

def _silu(x):
    return jax.nn.silu(x)

def _sigmoid(x):
    return jax.nn.sigmoid(x)

def _layernorm(x, axis=-1, eps=1e-05):
    m = jnp.mean(x, axis=axis, keepdims=True)
    v = jnp.var(x, axis=axis, keepdims=True)
    return (x - m) / jnp.sqrt(v + eps)

def _scatter_add(tgt, idx, src, axis=0):
    return tgt.at[idx].add(src)

def _segment_sum(src, seg, n):
    return jax.ops.segment_sum(src, seg, n)
kernel_name = 'mk_early_fusion_embed_d1_tok_img768_r4_eb2b1b'

def setup_inputs(seed: int=0):
    np.random.seed(seed)
    _w = jnp.asarray

    def _rec_inputs():
        import jax
        import jax.numpy as jnp
        _rk = jax.random.key(seed)
        x = -0.000125008 + 0.999885 * jax.random.normal(jax.random.fold_in(_rk, 1), (16, 2, 128, 128), jnp.float32)
        x_txt = jax.random.randint(jax.random.fold_in(_rk, 51), (16, 128), 0, 12564, jnp.int32)
        return (x, x_txt)
    x, x_txt = _rec_inputs()

    def _L0_tok_setup():
        import jax, jax.numpy as jnp
        import numpy as np
        PATCH = 16

        def _patchify(x, p):
            B, C, H, W = x.shape
            nh, nw = (H // p, W // p)
            patch_dim = C * p * p
            x = x.reshape(B, C, nh, p, nw, p)
            x = jnp.transpose(x, (0, 1, 2, 4, 3, 5))
            return x.reshape(B, -1, patch_dim)
        key = jax.random.key(seed)
        k1, k2, k3, k4 = jax.random.split(key, 4)
        B, C, H, W = (64, 2, 128, 128)
        dim = 192
        num_patches = H // PATCH * (W // PATCH)
        patch_dim = C * PATCH * PATCH
        x = jax.random.normal(k1, (B, C, H, W), dtype=jnp.float32)
        proj_w = jax.random.normal(k2, (dim, patch_dim), dtype=jnp.float32) * 0.02
        proj_b = jax.random.normal(k3, (dim,), dtype=jnp.float32) * 0.02
        pos_emb = jax.random.normal(k4, (1, num_patches, dim), dtype=jnp.float32) * 0.02
        return {'x': x, 'proj_w': proj_w, 'proj_b': proj_b, 'pos_emb': pos_emb}
    _L0_tok_all = _L0_tok_setup()
    _L0_tok_in = {k: v for k, v in _L0_tok_all.items() if k in ('proj_w', 'proj_b', 'pos_emb')}
    del _L0_tok_all

    def _L0_txt_setup():
        import jax, jax.numpy as jnp
        import numpy as np
        B, T, V, C = (8, 512, 50257, 192)

        def _rosa(x):
            Bx, Tx = x.shape
            eq = (x[:, :, None] == x[:, None, :]).astype(jnp.int32)

            def step(prev, eq_row):
                cur = (jnp.pad(prev[:, :-1], ((0, 0), (1, 0))) + 1) * eq_row
                return (cur, cur)
            init = jnp.zeros((Bx, Tx), jnp.int32)
            _, rows = jax.lax.scan(step, init, jnp.swapaxes(eq, 0, 1)[1:])
            L = jnp.swapaxes(jnp.concatenate([init[None], rows], axis=0), 0, 1)
            mask = jnp.tril(jnp.ones((Tx, Tx), dtype=bool), -1)
            j = jnp.arange(Tx, dtype=jnp.float32)
            TIE = 1e-05
            scored = jnp.where(mask[None], L.astype(jnp.float32) + j[None, None, :] * TIE, -1.0)
            best_j = jnp.argmax(scored, axis=2)
            pred_idx = jnp.minimum(best_j + 1, Tx - 1)
            preds = jnp.take_along_axis(x, pred_idx, axis=1)
            no_match = jnp.max(jnp.where(mask[None], L, 0), axis=2) == 0
            return jnp.where(no_match, -1, preds)
        key = jax.random.key(seed)
        k1, k2 = jax.random.split(key)
        idx = jax.random.randint(k1, (B, T), 0, V)
        emb = jax.random.normal(k2, (V, C), dtype=jnp.float32)
        return {'idx': idx, 'emb': emb}
    _L0_txt_all = _L0_txt_setup()
    _L0_txt_in = {k: v for k, v in _L0_txt_all.items() if k in ('emb',)}
    del _L0_txt_all

    def _L0_attn_setup():
        import jax, jax.numpy as jnp
        import numpy as np
        DIM = 192
        D_STATE = 16
        D_CONV = 4
        EXPAND = 2
        D_INNER = EXPAND * DIM
        DT_RANK = (DIM + 15) // 16
        B, L = (2, 512)
        EPS = 1e-05

        def layer_norm(x, g, b):
            mu = jnp.mean(x, axis=-1, keepdims=True)
            var = jnp.mean(jnp.square(x - mu), axis=-1, keepdims=True)
            return (x - mu) * jax.lax.rsqrt(var + EPS) * g + b

        def causal_conv1d(x, w, b):
            K = w.shape[1]
            xp = jnp.pad(x, ((0, 0), (K - 1, 0), (0, 0)))
            y = sum((xp[:, k:k + x.shape[1], :] * w[:, k] for k in range(K)))
            return y + b

        def selective_scan(u, dt, A, Bm, C, Dskip):
            dA = jnp.exp(jnp.einsum('bld,dn->bldn', dt, A))
            dBu = jnp.einsum('bld,bln->bldn', dt * u, Bm)

            def step(h, xs):
                dA_t, dBu_t, C_t = xs
                h = dA_t * h + dBu_t
                y = jnp.einsum('bdn,bn->bd', h, C_t)
                return (h, y)
            h0 = jnp.zeros((u.shape[0], A.shape[0], A.shape[1]), u.dtype)
            _, ys = jax.lax.scan(step, h0, (dA.transpose(1, 0, 2, 3), dBu.transpose(1, 0, 2, 3), C.transpose(1, 0, 2)))
            return ys.transpose(1, 0, 2) + u * Dskip

        def mamba_dir(xh, z, A_log, conv_w, conv_b, x_proj_w, dt_proj_w, dt_proj_b, Dskip):
            xc = jax.nn.silu(causal_conv1d(xh, conv_w, conv_b))
            x_dbl = jnp.einsum('bld,ed->ble', xc, x_proj_w)
            dt_r = x_dbl[..., :DT_RANK]
            Bm = x_dbl[..., DT_RANK:DT_RANK + D_STATE]
            C = x_dbl[..., DT_RANK + D_STATE:]
            dt = jax.nn.softplus(jnp.einsum('blr,dr->bld', dt_r, dt_proj_w) + dt_proj_b)
            A = -jnp.exp(A_log)
            y = selective_scan(xc, dt, A, Bm, C, Dskip)
            return y * jax.nn.silu(z)

        def mamba(x, in_proj_w, conv_w, conv_b, x_proj_w, dt_proj_w, dt_proj_b, A_log, A_b_log, Dskip, out_proj_w):
            xz = jnp.einsum('bld,ed->ble', x, in_proj_w)
            xh, z = (xz[..., :D_INNER], xz[..., D_INNER:])
            out_f = mamba_dir(xh, z, A_log, conv_w, conv_b, x_proj_w, dt_proj_w, dt_proj_b, Dskip)
            out_b = mamba_dir(xh[:, ::-1], z[:, ::-1], A_b_log, conv_w, conv_b, x_proj_w, dt_proj_w, dt_proj_b, Dskip)[:, ::-1]
            return jnp.einsum('bld,od->blo', out_f + out_b, out_proj_w)
        key = jax.random.key(seed)
        ks = jax.random.split(key, 10)
        s = 0.02
        f32 = jnp.float32
        A_init = jnp.log(jnp.tile(jnp.arange(1, D_STATE + 1, dtype=f32), (D_INNER, 1)))
        return {'x': jax.random.normal(ks[0], (B, L, DIM), f32), 'g1': jnp.ones((DIM,), f32), 'b1': jnp.zeros((DIM,), f32), 'in_proj_w': s * jax.random.normal(ks[1], (2 * D_INNER, DIM), f32), 'conv_w': s * jax.random.normal(ks[2], (D_INNER, D_CONV), f32), 'conv_b': jnp.zeros((D_INNER,), f32), 'x_proj_w': s * jax.random.normal(ks[3], (DT_RANK + 2 * D_STATE, D_INNER), f32), 'dt_proj_w': s * jax.random.normal(ks[4], (D_INNER, DT_RANK), f32), 'dt_proj_b': 0.01 * jnp.ones((D_INNER,), f32), 'A_log': A_init, 'A_b_log': A_init, 'Dskip': jnp.ones((D_INNER,), f32), 'out_proj_w': s * jax.random.normal(ks[5], (DIM, D_INNER), f32), 'g2': jnp.ones((DIM,), f32), 'b2': jnp.zeros((DIM,), f32), 'fc1_w': s * jax.random.normal(ks[6], (2 * DIM, DIM), f32), 'fc1_b': jnp.zeros((2 * DIM,), f32), 'fc2_w': s * jax.random.normal(ks[7], (DIM, 2 * DIM), f32), 'fc2_b': jnp.zeros((DIM,), f32)}
    _L0_attn_all = _L0_attn_setup()
    _L0_attn_in = {k: v for k, v in _L0_attn_all.items() if k in ('g1', 'b1', 'in_proj_w', 'conv_w', 'conv_b', 'x_proj_w', 'dt_proj_w', 'dt_proj_b', 'A_log', 'A_b_log', 'Dskip', 'out_proj_w', 'g2', 'b2', 'fc1_w', 'fc1_b', 'fc2_w', 'fc2_b')}
    del _L0_attn_all

    def _L0_ffn_setup():
        import jax, jax.numpy as jnp
        import numpy as np
        DEPTH = 11

        def _fff_forward(inputs, weights_in, weights_out, depth=DEPTH):
            B, S, _ = inputs.shape
            n_nodes = weights_in.shape[0]
            max_index = n_nodes - 1
            all_logits = jnp.einsum('bsd,nd->bsn', inputs, weights_in)

            def step(prev_idx, _):
                sel = jnp.clip(prev_idx, 0, max_index)
                logits = jnp.take_along_axis(all_logits, sel[..., None], axis=-1)[..., 0]
                new_idx = jnp.clip(2 * sel + 1 + (logits > 0).astype(sel.dtype), 0, max_index)
                return (new_idx, (logits, new_idx))
            idx0 = jnp.zeros((B, S), dtype=jnp.int32)
            _, (logits_seq, idx_seq) = jax.lax.scan(step, idx0, None, length=depth - 1)
            logits = jnp.concatenate([jnp.zeros((1, B, S), all_logits.dtype), logits_seq], axis=0)
            node_idx = jnp.concatenate([idx0[None], idx_seq], axis=0)
            act = jax.nn.gelu(logits, approximate=False)
            onehot = jax.nn.one_hot(node_idx, n_nodes, dtype=act.dtype)
            coeff = jnp.einsum('dbs,dbsn->bsn', act, onehot)
            return jnp.einsum('bsn,nd->bsd', coeff, weights_out)
        key = jax.random.key(seed)
        k1, k2, k3 = jax.random.split(key, 3)
        B, S, D = (4, 1024, 192)
        n_nodes = 2 * DEPTH - 1
        return {'inputs': jax.random.normal(k1, (B, S, D), dtype=jnp.float32), 'weights_in': jax.random.normal(k2, (n_nodes, D), dtype=jnp.float32), 'weights_out': jax.random.normal(k3, (n_nodes, D), dtype=jnp.float32)}
    _L0_ffn_all = _L0_ffn_setup()
    _L0_ffn_in = {k: v for k, v in _L0_ffn_all.items() if k in ('weights_in', 'weights_out')}
    del _L0_ffn_all
    return {'x': x, 'x_txt': x_txt, 'L0_tok_proj_w': _L0_tok_in['proj_w'], 'L0_tok_proj_b': _L0_tok_in['proj_b'], 'L0_tok_pos_emb': _L0_tok_in['pos_emb'], 'L0_txt_emb': _L0_txt_in['emb'], 'L0_attn_g1': _L0_attn_in['g1'], 'L0_attn_b1': _L0_attn_in['b1'], 'L0_attn_in_proj_w': _L0_attn_in['in_proj_w'], 'L0_attn_conv_w': _L0_attn_in['conv_w'], 'L0_attn_conv_b': _L0_attn_in['conv_b'], 'L0_attn_x_proj_w': _L0_attn_in['x_proj_w'], 'L0_attn_dt_proj_w': _L0_attn_in['dt_proj_w'], 'L0_attn_dt_proj_b': _L0_attn_in['dt_proj_b'], 'L0_attn_A_log': _L0_attn_in['A_log'], 'L0_attn_A_b_log': _L0_attn_in['A_b_log'], 'L0_attn_Dskip': _L0_attn_in['Dskip'], 'L0_attn_out_proj_w': _L0_attn_in['out_proj_w'], 'L0_attn_g2': _L0_attn_in['g2'], 'L0_attn_b2': _L0_attn_in['b2'], 'L0_attn_fc1_w': _L0_attn_in['fc1_w'], 'L0_attn_fc1_b': _L0_attn_in['fc1_b'], 'L0_attn_fc2_w': _L0_attn_in['fc2_w'], 'L0_attn_fc2_b': _L0_attn_in['fc2_b'], 'L0_ffn_weights_in': _L0_ffn_in['weights_in'], 'L0_ffn_weights_out': _L0_ffn_in['weights_out']}

def reference(x, x_txt, L0_tok_proj_w, L0_tok_proj_b, L0_tok_pos_emb, L0_txt_emb, L0_attn_g1, L0_attn_b1, L0_attn_in_proj_w, L0_attn_conv_w, L0_attn_conv_b, L0_attn_x_proj_w, L0_attn_dt_proj_w, L0_attn_dt_proj_b, L0_attn_A_log, L0_attn_A_b_log, L0_attn_Dskip, L0_attn_out_proj_w, L0_attn_g2, L0_attn_b2, L0_attn_fc1_w, L0_attn_fc1_b, L0_attn_fc2_w, L0_attn_fc2_b, L0_ffn_weights_in, L0_ffn_weights_out):
    import jax
    import jax.numpy as jnp

    def _L0_tok_ref(x, proj_w, proj_b, pos_emb):
        import jax, jax.numpy as jnp
        import numpy as np
        PATCH = 16

        def _patchify(x, p):
            B, C, H, W = x.shape
            nh, nw = (H // p, W // p)
            patch_dim = C * p * p
            x = x.reshape(B, C, nh, p, nw, p)
            x = jnp.transpose(x, (0, 1, 2, 4, 3, 5))
            return x.reshape(B, -1, patch_dim)
        patches = _patchify(x, PATCH)
        out = jnp.einsum('bnp,dp->bnd', patches, proj_w) + proj_b
        return out + pos_emb

    def _L0_txt_ref(idx, emb):
        import jax, jax.numpy as jnp
        import numpy as np
        B, T, V, C = (8, 512, 50257, 192)

        def _rosa(x):
            Bx, Tx = x.shape
            eq = (x[:, :, None] == x[:, None, :]).astype(jnp.int32)

            def step(prev, eq_row):
                cur = (jnp.pad(prev[:, :-1], ((0, 0), (1, 0))) + 1) * eq_row
                return (cur, cur)
            init = jnp.zeros((Bx, Tx), jnp.int32)
            _, rows = jax.lax.scan(step, init, jnp.swapaxes(eq, 0, 1)[1:])
            L = jnp.swapaxes(jnp.concatenate([init[None], rows], axis=0), 0, 1)
            mask = jnp.tril(jnp.ones((Tx, Tx), dtype=bool), -1)
            j = jnp.arange(Tx, dtype=jnp.float32)
            TIE = 1e-05
            scored = jnp.where(mask[None], L.astype(jnp.float32) + j[None, None, :] * TIE, -1.0)
            best_j = jnp.argmax(scored, axis=2)
            pred_idx = jnp.minimum(best_j + 1, Tx - 1)
            preds = jnp.take_along_axis(x, pred_idx, axis=1)
            no_match = jnp.max(jnp.where(mask[None], L, 0), axis=2) == 0
            return jnp.where(no_match, -1, preds)
        p = _rosa(idx)
        out = emb[jnp.clip(p, 0)]
        return jnp.where((p == -1)[..., None], 0.0, out)

    def _L0_attn_ref(x, g1, b1, in_proj_w, conv_w, conv_b, x_proj_w, dt_proj_w, dt_proj_b, A_log, A_b_log, Dskip, out_proj_w, g2, b2, fc1_w, fc1_b, fc2_w, fc2_b):
        import jax, jax.numpy as jnp
        import numpy as np
        DIM = 192
        D_STATE = 16
        D_CONV = 4
        EXPAND = 2
        D_INNER = EXPAND * DIM
        DT_RANK = (DIM + 15) // 16
        B, L = (2, 512)
        EPS = 1e-05

        def layer_norm(x, g, b):
            mu = jnp.mean(x, axis=-1, keepdims=True)
            var = jnp.mean(jnp.square(x - mu), axis=-1, keepdims=True)
            return (x - mu) * jax.lax.rsqrt(var + EPS) * g + b

        def causal_conv1d(x, w, b):
            K = w.shape[1]
            xp = jnp.pad(x, ((0, 0), (K - 1, 0), (0, 0)))
            y = sum((xp[:, k:k + x.shape[1], :] * w[:, k] for k in range(K)))
            return y + b

        def selective_scan(u, dt, A, Bm, C, Dskip):
            dA = jnp.exp(jnp.einsum('bld,dn->bldn', dt, A))
            dBu = jnp.einsum('bld,bln->bldn', dt * u, Bm)

            def step(h, xs):
                dA_t, dBu_t, C_t = xs
                h = dA_t * h + dBu_t
                y = jnp.einsum('bdn,bn->bd', h, C_t)
                return (h, y)
            h0 = jnp.zeros((u.shape[0], A.shape[0], A.shape[1]), u.dtype)
            _, ys = jax.lax.scan(step, h0, (dA.transpose(1, 0, 2, 3), dBu.transpose(1, 0, 2, 3), C.transpose(1, 0, 2)))
            return ys.transpose(1, 0, 2) + u * Dskip

        def mamba_dir(xh, z, A_log, conv_w, conv_b, x_proj_w, dt_proj_w, dt_proj_b, Dskip):
            xc = jax.nn.silu(causal_conv1d(xh, conv_w, conv_b))
            x_dbl = jnp.einsum('bld,ed->ble', xc, x_proj_w)
            dt_r = x_dbl[..., :DT_RANK]
            Bm = x_dbl[..., DT_RANK:DT_RANK + D_STATE]
            C = x_dbl[..., DT_RANK + D_STATE:]
            dt = jax.nn.softplus(jnp.einsum('blr,dr->bld', dt_r, dt_proj_w) + dt_proj_b)
            A = -jnp.exp(A_log)
            y = selective_scan(xc, dt, A, Bm, C, Dskip)
            return y * jax.nn.silu(z)

        def mamba(x, in_proj_w, conv_w, conv_b, x_proj_w, dt_proj_w, dt_proj_b, A_log, A_b_log, Dskip, out_proj_w):
            xz = jnp.einsum('bld,ed->ble', x, in_proj_w)
            xh, z = (xz[..., :D_INNER], xz[..., D_INNER:])
            out_f = mamba_dir(xh, z, A_log, conv_w, conv_b, x_proj_w, dt_proj_w, dt_proj_b, Dskip)
            out_b = mamba_dir(xh[:, ::-1], z[:, ::-1], A_b_log, conv_w, conv_b, x_proj_w, dt_proj_w, dt_proj_b, Dskip)[:, ::-1]
            return jnp.einsum('bld,od->blo', out_f + out_b, out_proj_w)
        h = mamba(layer_norm(x, g1, b1), in_proj_w, conv_w, conv_b, x_proj_w, dt_proj_w, dt_proj_b, A_log, A_b_log, Dskip, out_proj_w) + x
        m = layer_norm(h, g2, b2)
        m = jax.nn.gelu(jnp.einsum('bld,hd->blh', m, fc1_w) + fc1_b, approximate=False)
        m = jnp.einsum('blh,dh->bld', m, fc2_w) + fc2_b
        return m + h

    def _L0_ffn_ref(inputs, weights_in, weights_out):
        import jax, jax.numpy as jnp
        import numpy as np
        DEPTH = 11

        def _fff_forward(inputs, weights_in, weights_out, depth=DEPTH):
            B, S, _ = inputs.shape
            n_nodes = weights_in.shape[0]
            max_index = n_nodes - 1
            all_logits = jnp.einsum('bsd,nd->bsn', inputs, weights_in)

            def step(prev_idx, _):
                sel = jnp.clip(prev_idx, 0, max_index)
                logits = jnp.take_along_axis(all_logits, sel[..., None], axis=-1)[..., 0]
                new_idx = jnp.clip(2 * sel + 1 + (logits > 0).astype(sel.dtype), 0, max_index)
                return (new_idx, (logits, new_idx))
            idx0 = jnp.zeros((B, S), dtype=jnp.int32)
            _, (logits_seq, idx_seq) = jax.lax.scan(step, idx0, None, length=depth - 1)
            logits = jnp.concatenate([jnp.zeros((1, B, S), all_logits.dtype), logits_seq], axis=0)
            node_idx = jnp.concatenate([idx0[None], idx_seq], axis=0)
            act = jax.nn.gelu(logits, approximate=False)
            onehot = jax.nn.one_hot(node_idx, n_nodes, dtype=act.dtype)
            coeff = jnp.einsum('dbs,dbsn->bsn', act, onehot)
            return jnp.einsum('bsn,nd->bsd', coeff, weights_out)
        return _fff_forward(inputs, weights_in, weights_out)
    h = _L0_tok_ref(x, L0_tok_proj_w, L0_tok_proj_b, L0_tok_pos_emb)
    h = jnp.concatenate([h, _L0_txt_ref(x_txt, L0_txt_emb)], axis=1)
    h = h + _L0_attn_ref(_layernorm(h, axis=-1), L0_attn_g1, L0_attn_b1, L0_attn_in_proj_w, L0_attn_conv_w, L0_attn_conv_b, L0_attn_x_proj_w, L0_attn_dt_proj_w, L0_attn_dt_proj_b, L0_attn_A_log, L0_attn_A_b_log, L0_attn_Dskip, L0_attn_out_proj_w, L0_attn_g2, L0_attn_b2, L0_attn_fc1_w, L0_attn_fc1_b, L0_attn_fc2_w, L0_attn_fc2_b)
    h = h + _L0_ffn_ref(_layernorm(h, axis=-1), L0_ffn_weights_in, L0_ffn_weights_out)
    return h

_drawn_inputs = setup_inputs


def setup_inputs(seed=0):
    import zlib

    import numpy as np

    out = dict(_drawn_inputs(seed))
    spreads = {'L0_attn_g1': (1.0, 0.6),
     'L0_attn_b1': (0.0, 0.1),
     'L0_attn_conv_b': (0.0, 0.1),
     'L0_attn_dt_proj_b': (0.009999999776482582, 0.6),
     'L0_attn_Dskip': (1.0, 0.6),
     'L0_attn_g2': (1.0, 0.2),
     'L0_attn_b2': (0.0, 0.462),
     'L0_attn_fc1_b': (0.0, 0.1),
     'L0_attn_fc2_b': (0.0, 0.1)}
    factors = {'L0_attn_conv_w': 8.0,
     'L0_attn_x_proj_w': 33.433,
     'L0_attn_dt_proj_w': 64.0,
     'L0_attn_A_log': 64.0,
     'L0_attn_A_b_log': 200.0}
    for name, (base, spread) in spreads.items():
        noise = np.random.default_rng([zlib.crc32(name.encode()), seed]).standard_normal(out[name].shape)
        drawn = base * np.exp(spread * noise) if base else spread * noise
        out[name] = jnp.asarray(drawn.astype(out[name].dtype))
    for name, factor in factors.items():
        out[name] = (out[name] * factor).astype(out[name].dtype)
    return out
```

```python
from contextlib import ExitStack

import concourse.bass as bass
from concourse import mybir

F32 = mybir.dt.float32
BF16 = mybir.dt.bfloat16
I32 = mybir.dt.int32
ALU = mybir.AluOpType
ACT = mybir.ActivationFunctionType
AX = mybir.AxisListType

NSEQ, LIMG, LTXT = 16, 64, 128
L = LIMG + LTXT
DIM, INNER, STATE, RANK = 192, 384, 16, 12
HALF = DIM // 2
CH = INNER // 128
XD = 2 * STATE + RANK
PER = 2
COLS = PER * L
BLOCKS = NSEQ // PER
TILES = 3
PATCH = 16
FEAT = 2 * PATCH * PATCH
FK = FEAT // 128
TAPS = 4
UNITS = CH * 2 * 16
QUADS = UNITS // 4
NODES = 21
EPS = 1e-5
RING_W, RING_H, RING_A = 3, 12, 2
PRE_USES, POST_USES = 26, 15
MOVES = 12 * 16
XH, CONV_F, XPROJ_F, CONV_B, XPROJ_B, DT_F, GATE, DT_B, REP_F, REP_B = 0, 3, 6, 7, 10, 11, 14, 17, 20, 22
OUTP, NORM_T, FC1, FC2, FFF_T, LOGITS, COEF_T, FFF_OUT = 0, 2, 4, 7, 9, 11, 12, 13
POST_AT = {2: 0, 3: 1, 7: 2, 8: 3, 9: 4, 10: 5, 11: 6, 12: 7, 13: 8, 16: 9, 17: 10, 18: 11, 20: 12, 21: 13, 22: 14}


def build(nc, A, out):
    ctx = ExitStack()
    with ctx:
        def sb(name, shape, dt=F32):
            return ctx.enter_context(nc.sbuf_tensor(name, shape, dt))

        def sem(name):
            return ctx.enter_context(nc.semaphore(name))

        ident = sb("ident", [128, 128])
        sel_spread = sb("sel_spread", [96, 4, 128], BF16)
        sel_sum = sb("sel_sum", [128, 4, 32])
        sel_rep = sb("sel_rep", [XD, 2, 128])
        w_in = sb("w_in", [HALF, 2, 2 * INNER])
        w_x = sb("w_x", [128, CH, XD])
        w_dt = sb("w_dt", [XD, INNER])
        w_out = sb("w_out", [128, CH, DIM])
        w_fc1 = sb("w_fc1", [HALF, 2, INNER])
        w_fc2 = sb("w_fc2", [128, CH, DIM])
        w_fin = sb("w_fin", [HALF, 2, NODES])
        w_fout = sb("w_fout", [NODES, DIM])
        taps = sb("taps", [128, CH, TAPS])
        diag_tap = sb("diag_tap", [128, CH, TAPS, 128])
        diag_skip = sb("diag_skip", [128, CH, 128])
        chan = sb("chan", [128, 4, CH])
        gains = sb("gains", [HALF, 4, 2])
        fc2_bias = sb("fc2_bias", [128, DIM])
        a_log = sb("a_log", [128, 2, 48])
        mhalf = sb("mhalf", [128, TILES])
        h0 = sb("h0", [128, BLOCKS * TILES * DIM])
        nrm = sb("nrm", [128, TILES, DIM])
        x1T = sb("x1T", [HALF, 2, COLS])
        xh = sb("xh", [128, CH, COLS])
        t_e = sb("t_e", [128, CH, COLS])
        t_u = sb("t_u", [128, CH, COLS])
        t_l = sb("t_l", [128, CH, COLS])
        xc = sb("xc", [128, 2, 2, CH, COLS])
        gate = sb("gate", [128, 2, CH, COLS])
        xdbl = sb("xdbl", [XD, 2, COLS])
        parts = sb("parts", [128, 2, 3, CH * COLS], BF16)
        spread = sb("spread", [128, 2, 2, CH, 4 * COLS], BF16)
        rep = sb("rep", [128, 2, 2, 2, COLS])
        decay = sb("decay", [128, 2, RING_A, COLS])
        hring = sb("hring", [128, RING_H, COLS])
        yz = sb("yz", [128, CH, COLS])
        hh = sb("hh", [128, TILES, DIM])
        h1 = sb("h1", [128, TILES, DIM])
        pnrm = sb("pnrm", [128, TILES, DIM])
        pT = sb("pT", [HALF, 2, COLS])
        gl = sb("gl", [128, CH, COLS])
        st = sb("st", [128, TILES, 6])
        mean0 = sb("mean0", [128, BLOCKS * TILES])
        pad = sb("pad", [128, 1])
        rs0 = sb("rs0", [128, BLOCKS * TILES])
        mv1 = sb("mv1", [128, 2, TILES])
        ve = sb("ve", [128, TILES])
        rs1 = sb("rs1", [128, TILES])
        pst = sb("pst", [128, TILES, 6])
        pmv = sb("pmv", [128, 2, TILES])
        pve = sb("pve", [128, TILES])
        prs = sb("prs", [128, TILES])
        act_l = sb("act_l", [128, TILES, NODES])
        go_r = sb("go_r", [128, 2, TILES, NODES])
        go_l = sb("go_l", [128, 2, TILES, NODES])
        tree = sb("tree", [128, 2, TILES, NODES])
        tsum = sb("tsum", [128, 2, TILES])
        coefT = gl[0:NODES, 0, :]
        best = sb("best", [128, NSEQ])
        besti = sb("besti", [128, 2, NSEQ], I32)
        flag = sb("flag", [128, NSEQ])
        tok = sb("tok", [128, NSEQ], I32)
        boff = sb("boff", [128, NSEQ], I32)

        early = spread[:, :, :, :, :].rearrange("p a b c x -> p (a b c x)").bitcast(F32)
        shifted, plain, eq, run = (early[:, i * 2048:(i + 1) * 2048] for i in range(4))
        hflat = hring[:, :, :].rearrange("p a b -> p (a b)")
        patches = hflat[:, 0:FK * 1024].rearrange("p (k t) -> p k t", k=FK)
        pflat = parts[:, :, :, :].rearrange("p a b c -> p (a b c)").bitcast(F32)
        w_tok = pflat[:, 0:FK * DIM].rearrange("p (k d) -> p k d", k=FK)
        pos = pflat[:, 768:768 + DIM]
        tok_bias = pflat[:, 960:960 + DIM]
        jrow = pflat[:, 1152:1152 + LTXT]

        ps = ctx.enter_context(nc.psum_tensor("ps", [128, 8, 512], F32))
        DT = [ps[:, i, 0:COLS] for i in (0, 1)]
        BU = [ps[:, i, 0:COLS] for i in (2, 3, 4)]
        Y, PRE, POST = (ps[:, i, 0:COLS] for i in (5, 6, 7))

        S = {n: sem(n) for n in (
            "txt_loaded", "img_loaded", "w_loaded", "best_ready", "keyT_ready", "rosa_idx", "ids_lo",
            "ids_hi", "emb_lo", "emb_hi", "text_masked", "img_ready", "img_taken", "img_done", "consts_set",
            "key_ready", "exp_a", "a_ready", "diag_ready", "pro",
            "dt_filled", "bu_filled", "decay_ready", "bu_ready", "state_ready", "prod_ready", "reduced",
            "y_taken", "pre_full", "pre_free", "post_full", "post_free",
            "ln0_ve", "ln0_rs", "ln1_ve", "ln1_rs", "x1_ready", "pre_v",
            "soft_e", "soft_l", "dt_ready", "hi_ready", "rest_ready", "mid_ready", "lo_ready",
            "hh_ve", "hh_rs", "m_ready", "h1_ve", "h1_rs", "v_ready", "post_v", "act_ready", "coef_ready",
            "soft_v", "hh_u", "mean_kept", "hh_b", "h1_sum", "tree_v", "sent_f_dt", "sent_f_dtu", "sent_b_dt", "sent_b_dtu",
            "out_sent")}
        SENT = (("sent_f_dt", "sent_f_dtu"), ("sent_b_dt", "sent_b_dtu"))

        def at_least(eng, name, k, per, more):
            if isinstance(k, int) and k * per + more <= 0:
                return
            eng.wait_ge(S[name], k * per + more)

        def tile(k, t):
            return h0[:, bass.ds((k * TILES + t) * DIM, DIM)]

        def cols_of(a, t):
            if t < PER:
                return a[:, t * L + LIMG:(t + 1) * L]
            return a.rearrange("p (b l) -> p b l", b=PER)[:, :, 0:LIMG]

        def unit(n):
            return n // 32, n // 16 % 2, n % 16 // 4, n % 4

        sel_raw = t_u[0:96, :, :].rearrange("p c x -> p (c x)")[:, 0:4 * 128]
        WLOADS = [(sel_raw, "c_spread"), (sel_sum[:, :, :], "c_sum"), (sel_rep[:, :, :], "c_rep"),
                  (w_in[:, :, :], "w_in"), (w_x[:, :, :], "w_x"), (w_dt[:, :], "w_dt"), (w_out[:, :, :], "w_out"),
                  (w_fc1[:, :, :], "w_fc1"), (w_fc2[:, :, :], "w_fc2"), (w_fin[:, :, :], "w_fin"),
                  (w_fout[:, :], "w_fout"), (taps[:, :, :], "taps"), (chan[:, :, :], "chan"),
                  (gains[:, :, :], "gains"), (fc2_bias[:, :], "fc2_bias"), (a_log[:, :, :], "a_log")]

        block = ctx.enter_context(nc.Block())

        @block.sync
        def _(sp):
            xpad = A["x_pad"]
            sp.dma_start(shifted.rearrange("p (b i) -> p b i", b=NSEQ).bitcast(I32),
                         bass.AP(xpad.tensor, 0, [[1, 128], [2 * LTXT, NSEQ], [1, LTXT]])).then_inc(S["txt_loaded"], 16)
            sp.dma_start(plain.rearrange("p (b i) -> p b i", b=NSEQ).bitcast(I32),
                         bass.AP(xpad.tensor, LTXT, [[0, 128], [2 * LTXT, NSEQ], [1, LTXT]])).then_inc(S["txt_loaded"], 16)
            sp.dma_start(jrow, A["c_jrow"]).then_inc(S["txt_loaded"], 16)
            sp.dma_start(ident[:, :], A["c_ident"]).then_inc(S["txt_loaded"], 16)
            sp.dma_start(boff[:, :], A["c_boff"]).then_inc(S["txt_loaded"], 16)
            sp.dma_start(w_tok, A["w_tok"]).then_inc(S["img_loaded"], 16)
            sp.dma_start(pos, A["pos"]).then_inc(S["img_loaded"], 16)
            sp.dma_start(tok_bias, A["tok_bias"]).then_inc(S["img_loaded"], 16)
            sp.dma_start(patches, A["patches"]).then_inc(S["img_loaded"], 16)
            for dst, name in WLOADS:
                sp.dma_start(dst, A[name]).then_inc(S["w_loaded"], 16)

            def send_parts(kk, dr, i):
                at_least(sp, "lo_ready", kk, 4, 2 * dr + i + 1)
                at_least(sp, "bu_filled", kk, UNITS, -16 * (1 - dr))
                v = parts[:, i, :, :].rearrange("p s (c x) -> p s c x", c=CH)
                for s in range(3):
                    for q in range(4):
                        sp.dma_start(spread[32 * s:32 * s + 32, i, dr, :, q * COLS:(q + 1) * COLS],
                                     v[32 * q:32 * q + 32, s, :, :]).then_inc(S[SENT[dr][i]], 16)

            def store(kk):
                at_least(sp, "post_free", kk, POST_USES, POST_USES)
                for b in range(PER):
                    sp.dma_start(out[bass.ds(kk * PER + b, 1), LIMG:L, :].rearrange("b l d -> (b l) d"),
                                 h1[:, b, :]).then_inc(S["out_sent"], 16)
                    sp.dma_start(out[bass.ds(kk * PER + b, 1), 0:LIMG, :].rearrange("b l d -> (b l) d"),
                                 h1[b * LIMG:(b + 1) * LIMG, 2, :]).then_inc(S["out_sent"], 16)

            for dr in range(2):
                for i in range(2):
                    send_parts(0, dr, i)

            def body(k, pre, post):
                if pre:
                    for dr in range(2):
                        for i in range(2):
                            send_parts(k + 1, dr, i)
                if post:
                    store(k - 1)

            body(0, True, False)
            with sp.Fori(0, 2) as it:
                body(it * 2 + 1, True, True)
                body(it * 2 + 2, True, True)
            body(5, True, True)
            body(6, True, True)
            body(7, False, True)
            store(7)
            sp.wait_ge(S["out_sent"], BLOCKS * 64)

        @block.gpsimd
        def _(pool):
            g = nc.gpsimd
            g.memset(mhalf[:, :], -0.5).then_inc(S["consts_set"], 1)
            pool.wait_ge(S["rosa_idx"], 1)
            for b in range(NSEQ):
                g.indirect_dma_start(tok[:, b:b + 1], None, A["x_ids"],
                                     bass.IndirectOffsetOnAxis(besti[:, 1, b:b + 1], 0))\
                    .then_inc(S["ids_lo" if b < PER else "ids_hi"], 16)
            for b in range(NSEQ):
                if b == 0:
                    pool.wait_ge(S["ids_lo"], 16 * PER)
                if b == PER:
                    pool.wait_ge(S["ids_hi"], 16 * (NSEQ - PER))
                t = b // PER * TILES + b % PER
                g.indirect_dma_start(h0[:, t * DIM:(t + 1) * DIM], None, A["emb"],
                                     bass.IndirectOffsetOnAxis(tok[:, b:b + 1], 0))\
                    .then_inc(S["emb_lo" if b < PER else "emb_hi"], 16)

            def power(var, res, kk, ready, done, per=1):
                at_least(pool, ready, kk, 1, 1)
                g.tensor_tensor(res, var, mhalf[:, :], ALU.pow).then_inc(S[done], 1)

            def pre1(kk, step):
                if step == 0:
                    power(ve[:, :], rs0[:, bass.ds(kk * TILES, TILES)], kk, "ln0_ve", "ln0_rs")
                else:
                    power(ve[:, :], rs1[:, :], kk, "ln1_ve", "ln1_rs")

            def prod(k, par, n):
                c, dr, j, q = unit(n)
                at_least(pool, "state_ready", k, UNITS, n + 1)
                h = hring[:, n % RING_H, :]
                g.tensor_tensor(h, h, rep[:, par, dr, 1, :], ALU.mult).then_inc(S["prod_ready"], 1)

            def body(k, par, pre2, pre1_, post):
                for q in range(QUADS):
                    for n in range(4 * q, 4 * q + 4):
                        prod(k, par, n)
                    if pre1_ and q == 4:
                        pre1(k + 2, 0)
                    if pre1_ and q == 6:
                        pre1(k + 2, 1)
                    if post and q == 4:
                        power(pve[:, :], prs[:, :], k - 1, "hh_ve", "hh_rs")
                    if post and q == 13:
                        power(pve[:, :], prs[:, :], k - 1, "h1_ve", "h1_rs")

            pool.wait_ge(S["consts_set"], 1)
            pre1(0, 0)
            pre1(0, 1)
            pre1(1, 0)
            pre1(1, 1)
            body(0, 0, True, True, False)
            with pool.Fori(0, 2) as it:
                body(it * 2 + 1, 1, True, True, True)
                body(it * 2 + 2, 0, True, True, True)
            body(5, 1, True, True, True)
            body(6, 0, True, False, True)
            body(7, 1, False, False, True)
            power(pve[:, :], prs[:, :], 7, "hh_ve", "hh_rs")
            power(pve[:, :], prs[:, :], 7, "h1_ve", "h1_rs")

        @block.scalar
        def _(act):
            a = nc.scalar.activation
            act.wait_ge(S["exp_a"], 1)
            a(a_log[:, :, :], a_log[:, :, :], ACT.Exp).then_inc(S["a_ready"], 1)

            def full(name, kk, per, i):
                at_least(act, name, kk, per, i + 1)

            def pre1(kk, half):
                full("pre_full", kk, PRE_USES, half)
                a(x1T[:, half, :], PRE[0:HALF, :], ACT.Identity, scale=gains[:, 0, half:half + 1],
                  bias=gains[:, 1, half:half + 1]).then_inc(S["pre_free"], 1)

            def pre2(kk, par, u):
                if u < PRE_USES - 2:
                    full("pre_full", kk, PRE_USES, 2 + u)
                if u < CONV_F:
                    if u == 0:
                        at_least(act, "lo_ready", kk, 4, 0)
                    a(xh[:, u, :], PRE, ACT.Identity).then_inc(S["pre_free"], 1)
                elif u < XPROJ_F or CONV_B <= u < XPROJ_B:
                    dr, c = (0, u - CONV_F) if u < XPROJ_F else (1, u - CONV_B)
                    if c == 0 and dr == 0:
                        at_least(act, "reduced", kk, QUADS, -QUADS)
                    a(xc[:, par, dr, c, :], PRE, ACT.Silu, bias=chan[:, 0, c:c + 1]).then_inc(S["pre_free"], 1)
                elif u in (XPROJ_F, XPROJ_B):
                    a(xdbl[:, int(u == XPROJ_B), :], PRE[0:XD, :], ACT.Identity).then_inc(S["pre_free"], 1)
                elif DT_F <= u < GATE or DT_B <= u < REP_F:
                    dr, c = (0, u - DT_F) if u < GATE else (1, u - DT_B)
                    if c == 0:
                        at_least(act, "lo_ready", kk, 4, 2 * dr)
                    a(xh[:, c, :], PRE, ACT.Relu, bias=chan[:, 1, c:c + 1])
                    a(t_e[:, c, :], PRE, ACT.Abs, bias=chan[:, 1, c:c + 1]).then_inc(S["pre_free"], 1)
                    if c == CH - 1:
                        act.wait_ge(S["pre_free"], kk * PRE_USES + 2 + u + 1)
                        a(t_e[:, :, :], t_e[:, :, :], ACT.Exp, scale=-1.0).then_inc(S["soft_e"], 1)
                        act.wait_ge(S["soft_e"], kk * 2 + dr + 1)
                        a(t_u[:, :, :], t_e[:, :, :], ACT.Identity, bias=1.0)
                        a(t_l[:, :, :], t_e[:, :, :], ACT.Ln, bias=1.0).then_inc(S["soft_l"], 1)
                elif GATE <= u < DT_B:
                    c = u - GATE
                    if c == 0:
                        at_least(act, "y_taken", kk, CH, -CH)
                    a(gate[:, par, c, :], PRE, ACT.Silu).then_inc(S["pre_free"], 1)
                else:
                    dr, which = divmod(u - REP_F, 2)
                    if u == REP_F:
                        at_least(act, "prod_ready", kk, UNITS, -UNITS)
                    a(rep[:, par, dr, which, :], PRE, ACT.Identity).then_inc(S["pre_free"], 1)

            def split_hi(kk, dr):
                for i, src in enumerate((xh, t_e)):
                    at_least(act, "dt_ready", kk, 4, 2 * dr + i + 1)
                    at_least(act, SENT[1 - dr][i], kk, MOVES, (dr - 1) * MOVES + dr * MOVES)
                    a(parts[:, i, 0, :], src[:, :, :].rearrange("p c x -> p (c x)"), ACT.Identity)\
                        .then_inc(S["hi_ready"], 1)

            def split_mid(kk, dr):
                for i, src in enumerate((t_u, t_l)):
                    at_least(act, "rest_ready", kk, 4, 2 * dr + i + 1)
                    a(parts[:, i, 1, :], src[:, :, :].rearrange("p c x -> p (c x)"), ACT.Identity)\
                        .then_inc(S["mid_ready"], 1)

            def post(kk, u):
                if u in (NORM_T, NORM_T + 1):
                    full("post_full", kk, POST_USES, u)
                    half = u - NORM_T
                    a(pT[:, half, :], POST[0:HALF, :], ACT.Identity, scale=gains[:, 2, half:half + 1],
                      bias=gains[:, 3, half:half + 1]).then_inc(S["post_free"], 1)
                elif FC1 <= u < FC2:
                    full("post_full", kk, POST_USES, u)
                    c = u - FC1
                    a(gl[:, c, :], POST, ACT.Gelu, bias=chan[:, 3, c:c + 1]).then_inc(S["post_free"], 1)
                elif u in (FFF_T, FFF_T + 1):
                    full("post_full", kk, POST_USES, u)
                    a(pT[:, u - FFF_T, :], POST[0:HALF, :], ACT.Identity).then_inc(S["post_free"], 1)
                elif u == LOGITS:
                    full("post_full", kk, POST_USES, u)
                    a(act_l[:, :, :].rearrange("p t n -> p (t n)"), POST[:, 0:TILES * NODES], ACT.Gelu)\
                        .then_inc(S["act_ready"], 1)
                elif u == COEF_T:
                    full("post_full", kk, POST_USES, u)
                    a(coefT, POST[0:NODES, :], ACT.Identity).then_inc(S["post_free"], 1)

            def decay_of(k, n):
                c, dr, j, q = unit(n)
                at_least(act, "dt_filled", k, UNITS, n + 1)
                at_least(act, "state_ready", k, UNITS, n - RING_A + 1)
                g = c * 16 + q * 4 + j
                lo = 1 if dr == 0 else 0
                src = DT[n % 2].rearrange("p (b l) -> p b l", b=PER)[:, :, lo:lo + L - 1]
                dst = decay[:, dr, n % RING_A, :].rearrange("p (b l) -> p b l", b=PER)[:, :, lo:lo + L - 1]
                a(dst, src, ACT.Exp, scale=a_log[:, dr, g:g + 1]).then_inc(S["decay_ready"], 1)

            def body(k, par, pre, pre1_, post_):
                for q in range(QUADS):
                    for n in range(4 * q, 4 * q + 4):
                        decay_of(k, n)
                    if pre:
                        pre2(k + 1, 1 - par, q)
                        if q == DT_F + CH:
                            split_hi(k + 1, 0)
                        if q == DT_F + CH + 1:
                            split_mid(k + 1, 0)
                        if q == DT_B + CH:
                            split_hi(k + 1, 1)
                        if q == DT_B + CH + 1:
                            split_mid(k + 1, 1)
                    if post_ and q in POST_AT:
                        post(k - 1, POST_AT[q])
                if pre1_:
                    pre1(k + 2, 0)
                    pre1(k + 2, 1)

            act.wait_ge(S["diag_ready"], 1)
            act.wait_ge(S["w_loaded"], 16 * len(WLOADS))
            pre1(0, 0)
            pre1(0, 1)
            for u in range(24):
                pre2(0, 0, u)
                if u in (GATE - 1, REP_F - 1):
                    split_hi(0, int(u > GATE))
                    split_mid(0, int(u > GATE))
            pre1(1, 0)
            pre1(1, 1)
            body(0, 0, True, True, False)
            with act.Fori(0, 2) as it:
                body(it * 2 + 1, 1, True, True, True)
                body(it * 2 + 2, 0, True, True, True)
            body(5, 1, True, True, True)
            body(6, 0, True, False, True)
            body(7, 1, False, False, True)
            for u in range(POST_USES):
                post(7, u)

        @block.tensor
        def _(pe):
            mm = nc.tensor.matmul

            def pre_bank(kk, i):
                at_least(pe, "pre_free", kk, PRE_USES, i)

            def post_bank(kk, i):
                at_least(pe, "post_free", kk, POST_USES, i)

            def turn(bank, src, half, full):
                for t in range(TILES):
                    i = nc.tensor.transpose(cols_of(bank[0:HALF, :], t), src[:, t, half * HALF:(half + 1) * HALF],
                                            ident[:, :])
                i.then_inc(S[full], 1)

            def pre1(kk, half):
                if half == 0:
                    at_least(pe, "x1_ready", kk, 1, 1)
                pre_bank(kk, half)
                turn(PRE, nrm, half, "pre_full")

            def conv(dr, par, c):
                for s in range(TAPS):
                    o, i = (slice(s, L), slice(0, L - s)) if dr == 0 else (slice(0, L - s), slice(s, L))
                    last = mm(PRE.rearrange("p (b l) -> p b l", b=PER)[:, :, o], diag_tap[:, c, TAPS - 1 - s, :],
                              xh[:, c, :].rearrange("p (b l) -> p b l", b=PER)[:, :, i],
                              start=(s == 0), stop=(s == TAPS - 1))
                return last

            def pre2(kk, par, u):
                pre_bank(kk, 2 + u)
                if u < CONV_F or GATE <= u < DT_B:
                    e = u if u < CONV_F else CH + u - GATE
                    for half in range(2):
                        last = mm(PRE, w_in[:, half, e * 128:(e + 1) * 128], x1T[:, half, :],
                                  start=(half == 0), stop=(half == 1))
                elif u < XPROJ_F:
                    last = conv(0, par, u - CONV_F)
                elif CONV_B <= u < XPROJ_B:
                    last = conv(1, par, u - CONV_B)
                elif u in (XPROJ_F, XPROJ_B):
                    dr = int(u == XPROJ_B)
                    for c in range(CH):
                        last = mm(PRE[0:XD, :], w_x[:, c, :], xc[:, par, dr, c, :], start=(c == 0), stop=(c == CH - 1))
                elif DT_F <= u < REP_F:
                    dr, c = (0, u - DT_F) if u < GATE else (1, u - DT_B)
                    last = mm(PRE, w_dt[:, c * 128:(c + 1) * 128], xdbl[:, dr, :], start=True, stop=True)
                else:
                    dr, which = divmod(u - REP_F, 2)
                    last = mm(PRE, sel_rep[:, which, :], xdbl[:, dr, :], start=True, stop=True)
                last.then_inc(S["pre_full"], 1)

            def by_token(col, width, t, terms):
                for b in range(1 if t < PER else PER):
                    rows, at = (slice(0, 128), t * L + LIMG) if t < PER else (slice(b * LIMG, (b + 1) * LIMG), b * L)
                    for i, (x, w) in enumerate(terms):
                        last = mm(ps[rows, 7, col:col + width], x[:, at:at + rows.stop - rows.start], w,
                                  start=(i == 0), stop=(i == len(terms) - 1), tile_position=(0, rows.start))
                return last

            def tokens(kk, u, src, w, tiles):
                post_bank(kk, u)
                for o, t in enumerate(tiles):
                    last = by_token(o * DIM, DIM, t, [(src[:, c, :], w[:, c, :]) for c in range(CH)])
                last.then_inc(S["post_full"], 1)

            def post(kk, u):
                if u in (OUTP, OUTP + 1):
                    at_least(pe, "y_taken", kk, CH, CH)
                    tokens(kk, u, yz, w_out, (0, 1) if u == OUTP else (2,))
                elif u in (NORM_T, NORM_T + 1):
                    at_least(pe, "m_ready", kk, 1, 1)
                    post_bank(kk, u)
                    turn(POST, pnrm, u - NORM_T, "post_full")
                elif FC1 <= u < FC2:
                    post_bank(kk, u)
                    c = u - FC1
                    for half in range(2):
                        last = mm(POST, w_fc1[:, half, c * 128:(c + 1) * 128], pT[:, half, :],
                                  start=(half == 0), stop=(half == 1))
                    last.then_inc(S["post_full"], 1)
                elif u in (FC2, FC2 + 1):
                    tokens(kk, u, gl, w_fc2, (0, 1) if u == FC2 else (2,))
                elif u in (FFF_T, FFF_T + 1):
                    at_least(pe, "v_ready", kk, 1, 1)
                    post_bank(kk, u)
                    turn(POST, pnrm, u - FFF_T, "post_full")
                elif u == LOGITS:
                    post_bank(kk, u)
                    for t in range(TILES):
                        last = by_token(t * NODES, NODES, t, [(pT[:, i, :], w_fin[:, i, :]) for i in range(2)])
                    last.then_inc(S["post_full"], 1)
                elif u == COEF_T:
                    at_least(pe, "coef_ready", kk, 1, 1)
                    post_bank(kk, u)
                    for t in range(TILES):
                        last = nc.tensor.transpose(ps[0:NODES, 7, t * 128:(t + 1) * 128], tree[:, 1, t, :], ident[:, :])
                    last.then_inc(S["post_full"], 1)
                else:
                    post_bank(kk, u)
                    for o, t in enumerate((0, 1) if u == FFF_OUT else (2,)):
                        last = mm(ps[:, 7, o * DIM:(o + 1) * DIM], coefT[:, t * 128:(t + 1) * 128], w_fout[:, :],
                                  start=True, stop=True)
                    last.then_inc(S["post_full"], 1)

            def spread_of(k, n):
                c, dr, j, q = unit(n)
                if n in (0, 16):
                    for i in range(2):
                        at_least(pe, SENT[dr][i], k, MOVES, MOVES)
                at_least(pe, "decay_ready", k, UNITS, n - 1)
                mm(DT[n % 2], sel_spread[:, j, :], spread[0:96, 0, dr, c, q * COLS:(q + 1) * COLS],
                   start=True, stop=True).then_inc(S["dt_filled"], 1)
                at_least(pe, "state_ready", k, UNITS, n - RING_W + 1)
                mm(BU[n % RING_W], sel_spread[:, j, :], spread[0:96, 1, dr, c, q * COLS:(q + 1) * COLS],
                   start=True, stop=True).then_inc(S["bu_filled"], 1)

            def reduce(k, par, quad):
                c, dr, j, _ = unit(4 * quad)
                if quad % 8 == 0:
                    at_least(pe, "y_taken", k, CH, c)
                    for d in range(2):
                        mm(Y, diag_skip[:, c, :], xc[:, par, d, c, :], start=(d == 0), stop=False)
                at_least(pe, "prod_ready", k, UNITS, 4 * quad + 4)
                for q in range(4):
                    last = mm(ps[32 * q:32 * q + 32, 5, 0:COLS], sel_sum[:, j, :], hring[:, (4 * quad + q) % RING_H, :],
                              start=False, stop=(quad % 8 == 7), tile_position=(0, 32 * q))
                last.then_inc(S["reduced"], 1)

            def body(k, par, pre, pre1_, post_):
                for q in range(QUADS):
                    for n in range(4 * q, 4 * q + 4):
                        spread_of(k, n)
                    if q >= 2:
                        reduce(k, par, q - 2)
                    elif not (isinstance(k, int) and k == 0):
                        reduce(k - 1, 1 - par, QUADS - 2 + q)
                    if pre:
                        pre2(k + 1, 1 - par, q)
                    if post_ and q in POST_AT:
                        post(k - 1, POST_AT[q])
                if pre1_:
                    pre1(k + 2, 0)
                    pre1(k + 2, 1)

            pe.wait_ge(S["txt_loaded"], 5 * 16)
            pe.wait_ge(S["key_ready"], 1)
            for b in range(NSEQ):
                last = nc.tensor.transpose(ps[:, b // 4, b % 4 * 128:(b % 4 + 1) * 128], run[:, b * 128:(b + 1) * 128],
                                           ident[:, :])
            last.then_inc(S["keyT_ready"], 1)
            pe.wait_ge(S["img_loaded"], 4 * 16)
            for k in range(BLOCKS):
                if k >= 2:
                    pe.wait_ge(S["img_taken"], k - 1)
                for f in range(FK):
                    last = mm(ps[:, 4 + k % 2, 0:DIM], patches[:, f, k * 128:(k + 1) * 128], w_tok[:, f, :],
                              start=(f == 0), stop=(f == FK - 1))
                last.then_inc(S["img_ready"], 1)
            pe.wait_ge(S["w_loaded"], 16 * len(WLOADS))
            pe.wait_ge(S["diag_ready"], 1)
            pre1(0, 0)
            pre1(0, 1)
            for u in range(24):
                pre2(0, 0, u)
            pre1(1, 0)
            pre1(1, 1)
            pe.wait_ge(S["img_taken"], BLOCKS)
            body(0, 0, True, True, False)
            with pe.Fori(0, 2) as it:
                body(it * 2 + 1, 1, True, True, True)
                body(it * 2 + 2, 0, True, True, True)
            body(5, 1, True, True, True)
            body(6, 0, True, False, True)
            body(7, 1, False, False, True)
            reduce(7, 1, QUADS - 2)
            reduce(7, 1, QUADS - 1)
            for u in range(POST_USES):
                post(7, u)

        @block.vector
        def _(dve):
            v = nc.vector

            class Steps:

                def __init__(self, name, per):
                    self.name, self.per, self.n = name, per, 0

                def done(self, ins, kk):
                    self.n += 1
                    ins.then_inc(S[self.name], 1)
                    dve.wait_ge(S[self.name], kk * self.per + self.n)

            once = Steps("pro", 0)
            v.memset(decay[:, :, :, :], 0.0)
            v.memset(tree[:, :, :, :], 0.0)
            dve.wait_ge(S["txt_loaded"], 5 * 16)
            once.done(v.tensor_tensor(eq, shifted.bitcast(I32), plain.bitcast(I32), ALU.is_equal), 0)
            once.done(v.memset(shifted, 1.0), 0)
            once.done(v.tensor_tensor_scan(run, shifted, eq, 0.0, ALU.add, ALU.mult), 0)
            js = jrow.rearrange("p (o i) -> p o i", o=1).broadcast_to([128, NSEQ, LTXT])
            as3 = lambda x: x.rearrange("p (b i) -> p b i", b=NSEQ)
            once.done(v.scalar_tensor_tensor(as3(shifted), as3(run), 128.0, js, ALU.mult, ALU.add), 0)
            v.tensor_tensor(run, shifted, eq, ALU.mult).then_inc(S["key_ready"], 1)
            dve.wait_ge(S["w_loaded"], 16 * len(WLOADS))
            v.tensor_scalar(a_log[:, :, :], a_log[:, :, :], 80.0, None, ALU.min).then_inc(S["exp_a"], 1)
            v.tensor_copy(sel_spread[:, :, :].rearrange("p j m -> p (j m)"), sel_raw)
            for c in range(CH):
                for k in range(TAPS):
                    v.tensor_scalar(diag_tap[:, c, k, :], ident[:, :], taps[:, c, k:k + 1], None, ALU.mult)
                v.tensor_scalar(diag_skip[:, c, :], ident[:, :], chan[:, 2, c:c + 1], None, ALU.mult)
            dve.wait_ge(S["a_ready"], 1)
            v.tensor_scalar(a_log[:, :, :], a_log[:, :, :], -1.0, None, ALU.mult).then_inc(S["diag_ready"], 1)
            dve.wait_ge(S["keyT_ready"], 1)
            once.done(v.tensor_reduce(best[:, :], ps[:, 0:4, :].rearrange("p a (b j) -> p (a b) j", j=128), AX.X,
                                      ALU.max), 0)
            v.tensor_scalar(flag[:, :], best[:, :], 128.0, None, ALU.is_ge)
            once.done(v.tensor_copy(besti[:, 0, :], best[:, :]), 0)
            once.done(v.tensor_scalar(besti[:, 0, :], besti[:, 0, :], 127, None, ALU.bitwise_and), 0)
            v.tensor_tensor(besti[:, 1, :], besti[:, 0, :], boff[:, :], ALU.add).then_inc(S["rosa_idx"], 1)
            dve.wait_ge(S["img_loaded"], 4 * 16)
            once.done(v.tensor_tensor(pos, pos, tok_bias, ALU.add), 0)
            for k in range(BLOCKS):
                dve.wait_ge(S["img_ready"], k + 1)
                v.tensor_tensor(tile(k, 2), ps[:, 4 + k % 2, 0:DIM], pos, ALU.add).then_inc(S["img_taken"], 1)
            dve.wait_ge(S["img_taken"], BLOCKS)

            def mask_text(b0, b1):
                for b in range(b0, b1):
                    x = tile(b // PER, b % PER)
                    last = v.tensor_scalar(x, x, flag[:, b:b + 1], None, ALU.mult)
                last.then_inc(S["text_masked"], 1)

            PRE_V = 5

            def after(sem_name, value):
                dve.wait_ge(S[sem_name], value)
                v.memset(pad[:, :], 0.0)

            def pre1(kk, step):
                if step == 0:
                    for t in range(TILES):
                        last = v.bn_stats(st[:, t, :], tile(kk, t))
                    last.then_inc(S["pre_v"], 1)
                    after("pre_v", kk * PRE_V + 1)
                    for t in range(TILES):
                        last = v.bn_aggr(mv1[:, :, t], st[:, t, :])
                    last.then_inc(S["pre_v"], 1)
                    dve.wait_ge(S["pre_v"], kk * PRE_V + 2)
                    v.tensor_copy(mean0[:, bass.ds(kk * TILES, TILES)], mv1[:, 0, :]).then_inc(S["mean_kept"], 1)
                    v.tensor_scalar(ve[:, :], mv1[:, 1, :], EPS, None, ALU.add).then_inc(S["ln0_ve"], 1)
                elif step == 1:
                    at_least(dve, "ln0_rs", kk, 1, 1)
                    at_least(dve, "mean_kept", kk, 1, 1)
                    at_least(dve, "pre_full", kk, PRE_USES, -PRE_USES + 2)
                    for t in range(TILES):
                        last = v.tensor_scalar(nrm[:, t, :], tile(kk, t), mean0[:, bass.ds(kk * TILES + t, 1)],
                                               rs0[:, bass.ds(kk * TILES + t, 1)], ALU.subtract, ALU.mult)
                    last.then_inc(S["pre_v"], 1)
                    dve.wait_ge(S["pre_v"], kk * PRE_V + 3)
                    for t in range(TILES):
                        last = v.bn_stats(st[:, t, :], nrm[:, t, :])
                    last.then_inc(S["pre_v"], 1)
                    after("pre_v", kk * PRE_V + 4)
                    for t in range(TILES):
                        last = v.bn_aggr(mv1[:, :, t], st[:, t, :])
                    last.then_inc(S["pre_v"], 1)
                    dve.wait_ge(S["pre_v"], kk * PRE_V + 5)
                    v.tensor_scalar(ve[:, :], mv1[:, 1, :], EPS, None, ALU.add).then_inc(S["ln1_ve"], 1)
                else:
                    at_least(dve, "ln1_rs", kk, 1, 1)
                    for t in range(TILES):
                        last = v.tensor_scalar(nrm[:, t, :], nrm[:, t, :], mv1[:, 0, t:t + 1], rs1[:, t:t + 1],
                                               ALU.subtract, ALU.mult)
                    last.then_inc(S["x1_ready"], 1)

            def soft(kk, par, dr):
                at_least(dve, "soft_l", kk, 2, dr + 1)
                f = lambda x: x[:, :, :].rearrange("p c x -> p (c x)")
                base = kk * 4 + 2 * dr
                v.scalar_tensor_tensor(f(t_u), f(t_u), -1.0, f(t_e), ALU.add, ALU.subtract).then_inc(S["soft_v"], 1)
                dve.wait_ge(S["soft_v"], base + 1)
                v.tensor_tensor(f(t_l), f(t_l), f(t_u), ALU.subtract).then_inc(S["soft_v"], 1)
                dve.wait_ge(S["soft_v"], base + 2)
                v.tensor_tensor(f(xh), f(xh), f(t_l), ALU.add).then_inc(S["dt_ready"], 1)
                dve.wait_ge(S["dt_ready"], base + 1)
                v.tensor_tensor(f(t_e), f(xh), xc[:, par, dr, :, :].rearrange("p c x -> p (c x)"), ALU.mult)\
                    .then_inc(S["dt_ready"], 1)

            def rest(kk, dr):
                f = lambda x: x[:, :, :].rearrange("p c x -> p (c x)")
                for i, (src, dst) in enumerate(((xh, t_u), (t_e, t_l))):
                    at_least(dve, "hi_ready", kk, 4, 2 * dr + i + 1)
                    v.tensor_tensor(f(dst), f(src), parts[:, i, 0, :], ALU.subtract).then_inc(S["rest_ready"], 1)

            def low(kk, dr):
                f = lambda x: x[:, :, :].rearrange("p c x -> p (c x)")
                for i, src in enumerate((t_u, t_l)):
                    at_least(dve, "mid_ready", kk, 4, 2 * dr + i + 1)
                    v.tensor_tensor(parts[:, i, 2, :], f(src), parts[:, i, 1, :], ALU.subtract)\
                        .then_inc(S["lo_ready"], 1)

            def take_y(k, par, c):
                at_least(dve, "reduced", k, QUADS, 8 * c + 8)
                if c == 0:
                    at_least(dve, "post_full", k, POST_USES, OUTP + 2 - POST_USES)
                v.tensor_tensor(yz[:, c, :], Y, gate[:, par, c, :], ALU.mult).then_inc(S["y_taken"], 1)

            POST_V = 5

            def two(x, u, first):
                return x[:, 0:2, :] if u == first else x[:, 2:3, :]

            def bank(u, first):
                n = 2 if u == first else 1
                return ps[:, 7, 0:n * DIM].rearrange("p (t d) -> p t d", d=DIM)

            def post(kk, u):
                if u in (OUTP, OUTP + 1):
                    at_least(dve, "post_full", kk, POST_USES, u + 1)
                    tiles = (0, 1) if u == OUTP else (2,)
                    for t in tiles:
                        last = v.tensor_scalar(hh[:, t, :], tile(kk, t), mean0[:, bass.ds(kk * TILES + t, 1)],
                                               rs0[:, bass.ds(kk * TILES + t, 1)], ALU.subtract, ALU.mult)
                    last.then_inc(S["hh_u"], 1)
                    dve.wait_ge(S["hh_u"], kk * 2 + u + 1)
                    x = two(hh, u, OUTP)
                    v.tensor_tensor(x, bank(u, OUTP), x, ALU.add).then_inc(S["post_free"], 1)
                elif u in (FC2, FC2 + 1):
                    at_least(dve, "post_full", kk, POST_USES, u + 1)
                    at_least(dve, "out_sent", kk, 64, 0)
                    x = two(h1, u, FC2)
                    v.tensor_tensor(x, bank(u, FC2), two(hh, u, FC2), ALU.add).then_inc(S["post_free"], 1)
                    dve.wait_ge(S["post_free"], kk * POST_USES + u + 1)
                    n = 2 if u == FC2 else 1
                    t = 0 if u == FC2 else 2
                    v.tensor_tensor(x, x, h0[:, bass.ds((kk * TILES + t) * DIM, n * DIM)]
                                    .rearrange("p (t d) -> p t d", d=DIM), ALU.add).then_inc(S["h1_sum"], 1)
                elif u in (FFF_OUT, FFF_OUT + 1):
                    at_least(dve, "post_full", kk, POST_USES, u + 1)
                    x = two(h1, u, FFF_OUT)
                    v.tensor_tensor(x, bank(u, FFF_OUT), x, ALU.add).then_inc(S["post_free"], 1)

            def post_norm(kk, which, part):
                src = (hh, h1)[which]
                base = kk * 4 + 2 * which
                if part == 0:
                    if which == 0:
                        at_least(dve, "post_free", kk, POST_USES, OUTP + 2)
                    else:
                        at_least(dve, "h1_sum", kk, 2, 2)
                    for t in range(TILES):
                        last = v.bn_stats(pst[:, t, :], src[:, t, :])
                    last.then_inc(S["post_v"], 1)
                    after("post_v", base + 1)
                    for t in range(TILES):
                        last = v.bn_aggr(pmv[:, :, t], pst[:, t, :])
                    last.then_inc(S["post_v"], 1)
                    dve.wait_ge(S["post_v"], base + 2)
                    v.tensor_scalar(pve[:, :], pmv[:, 1, :], EPS, None, ALU.add)\
                        .then_inc(S[("hh_ve", "h1_ve")[which]], 1)
                else:
                    at_least(dve, ("hh_rs", "h1_rs")[which], kk, 1, 1)
                    for t in range(TILES):
                        last = v.tensor_scalar(pnrm[:, t, :], src[:, t, :], pmv[:, 0, t:t + 1], prs[:, t:t + 1],
                                               ALU.subtract, ALU.mult)
                    last.then_inc(S[("m_ready", "v_ready")[which]], 1)
                    if which == 0:
                        dve.wait_ge(S["m_ready"], kk + 1)
                        v.tensor_tensor(hh[:, :, :], hh[:, :, :], fc2_bias[:, :].rearrange("p (o d) -> p o d", o=1)
                                        .broadcast_to([128, TILES, DIM]), ALU.add).then_inc(S["hh_b"], 1)
                        dve.wait_ge(S["hh_b"], kk + 1)

            TREE_V = 11

            def walk(kk):
                s = Steps("tree_v", TREE_V)
                reached, coef = tree[:, 0, :, :], tree[:, 1, :, :]
                at_least(dve, "act_ready", kk, 1, 1)
                v.tensor_scalar(go_r[:, 0, :, :], ps[:, 7, 0:TILES * NODES].rearrange("p (t n) -> p t n", n=NODES),
                                0.0, None, ALU.is_gt).then_inc(S["post_free"], 1)
                dve.wait_ge(S["post_free"], kk * POST_USES + LOGITS + 1)
                s.done(v.tensor_scalar(go_l[:, 0, :, :], go_r[:, 0, :, :], -1.0, 1.0, ALU.mult, ALU.add), kk)
                v.tensor_tensor(go_r[:, 1, :, :], go_r[:, 0, :, :], act_l[:, :, :], ALU.mult)
                s.done(v.tensor_tensor(go_l[:, 1, :, :], go_l[:, 0, :, :], act_l[:, :, :], ALU.mult), kk)
                v.tensor_copy(tree[:, :, :, 1:2], go_l[:, :, :, 0:1])
                s.done(v.tensor_copy(tree[:, :, :, 2:3], go_r[:, :, :, 0:1]), kk)

                def level(n0, n1):
                    m = tree[:, 0:1, :, n0:n1].broadcast_to([128, 2, TILES, n1 - n0])
                    for off, go in ((1, go_l), (2, go_r)):
                        last = v.tensor_tensor(tree[:, :, :, 2 * n0 + off:2 * n1 + off - 1:2], m, go[:, :, :, n0:n1],
                                               ALU.mult)
                    s.done(last, kk)

                level(1, 3)
                level(3, 7)
                level(7, 10)
                s.done(v.tensor_reduce(tsum[:, 0, :], reached[:, :, 10:15], AX.X, ALU.add), kk)
                s.done(v.tensor_tensor(reached[:, :, 20], reached[:, :, 20], tsum[:, 0, :], ALU.add), kk)
                s.done(v.tensor_tensor(go_r[:, 0, :, 10:21], reached[:, :, 10:21], act_l[:, :, 10:21], ALU.mult), kk)
                s.done(v.tensor_reduce(tsum[:, 1, :], go_r[:, 0, :, 10:21], AX.X, ALU.add), kk)
                s.done(v.tensor_tensor(coef[:, :, 20], coef[:, :, 20], tsum[:, 1, :], ALU.add), kk)
                v.scalar_tensor_tensor(coef[:, :, 20], act_l[:, :, 20], 5.0, coef[:, :, 20], ALU.mult, ALU.add)\
                    .then_inc(S["coef_ready"], 1)
                assert s.n == TREE_V, s.n

            def times_b(k, par, n):
                c, dr, j, q = unit(n)
                at_least(dve, "bu_filled", k, UNITS, n + 1)
                if n in (0, 16):
                    at_least(dve, "pre_free", k, PRE_USES, 2 + REP_F + 2 * dr + 2)
                b = BU[n % RING_W]
                v.tensor_tensor(b, b, rep[:, par, dr, 0, :], ALU.mult).then_inc(S["bu_ready"], 1)

            def scan(k, n):
                c, dr, j, q = unit(n)
                at_least(dve, "decay_ready", k, UNITS, n + 1)
                if n % 4 == 0:
                    at_least(dve, "reduced", k, QUADS, n // 4 - 2)
                at_least(dve, "bu_ready", k, UNITS, n + 1)
                way = slice(None, None, 1 if dr == 0 else -1)
                v.tensor_tensor_scan(hring[:, n % RING_H, :][:, way], decay[:, dr, n % RING_A, :][:, way],
                                     BU[n % RING_W][:, way], 0.0, ALU.mult, ALU.add).then_inc(S["state_ready"], 1)

            def body(k, par, pre, pre1_, post_):
                for q in range(QUADS):
                    for n in range(4 * q, 4 * q + 4):
                        times_b(k, par, n)
                        if n:
                            scan(k, n - 1)
                        elif not (isinstance(k, int) and k == 0):
                            scan(k - 1, UNITS - 1)
                    if q % 8 == 1:
                        if q > 1:
                            take_y(k, par, q // 8 - 1)
                        elif not (isinstance(k, int) and k == 0):
                            take_y(k - 1, 1 - par, CH - 1)
                    if pre:
                        for dr, h in ((0, DT_F + CH), (1, DT_B + CH)):
                            if q == h:
                                soft(k + 1, 1 - par, dr)
                            if q == h + 1:
                                rest(k + 1, dr)
                            if q == h + 2:
                                low(k + 1, dr)
                    if pre1_ and q in (4, 6, 9):
                        pre1(k + 2, (4, 6, 9).index(q))
                    if post_:
                        if q in POST_AT:
                            post(k - 1, POST_AT[q])
                        if q == 4:
                            post_norm(k - 1, 0, 0)
                        if q == 6:
                            post_norm(k - 1, 0, 1)
                        if q == 13:
                            post_norm(k - 1, 1, 0)
                        if q == 15:
                            post_norm(k - 1, 1, 1)
                        if q == 19:
                            walk(k - 1)

            dve.wait_ge(S["emb_lo"], 16 * PER)
            mask_text(0, PER)
            dve.wait_ge(S["text_masked"], 1)
            for step in range(3):
                pre1(0, step)
            dve.wait_ge(S["emb_hi"], 16 * (NSEQ - PER))
            mask_text(PER, NSEQ)
            dve.wait_ge(S["text_masked"], 2)
            for dr in range(2):
                soft(0, 0, dr)
                rest(0, dr)
                low(0, dr)
            for step in range(3):
                pre1(1, step)
            body(0, 0, True, True, False)
            with dve.Fori(0, 2) as it:
                body(it * 2 + 1, 1, True, True, True)
                body(it * 2 + 2, 0, True, True, True)
            body(5, 1, True, True, True)
            body(6, 0, True, False, True)
            body(7, 1, False, False, True)
            scan(7, UNITS - 1)
            take_y(7, 1, CH - 1)
            post(7, OUTP)
            post(7, OUTP + 1)
            post_norm(7, 0, 0)
            post_norm(7, 0, 1)
            post(7, FC2)
            post(7, FC2 + 1)
            post_norm(7, 1, 0)
            post_norm(7, 1, 1)
            walk(7)
            post(7, FFF_OUT)
            post(7, FFF_OUT + 1)


def constants():
    import numpy as np

    spread = np.zeros((3, 32, 4, STATE, 8), np.float32)
    total = np.zeros((STATE, 8, 4, 32), np.float32)
    for j in range(4):
        for d in range(8):
            spread[:, 8 * j + d, j, :, d] = 1
            total[:, d, j, 8 * j + d] = 1
    rep = np.zeros((XD, 2, STATE, 8), np.float32)
    for n in range(STATE):
        rep[n, 0, n, :] = 1
        rep[STATE + n, 1, n, :] = 1
    pos = np.arange(LTXT)
    return {
        "c_spread": spread.reshape(96, 4 * 128), "c_sum": total.reshape(128, 4, 32),
        "c_rep": rep.reshape(XD, 2, 128), "c_ident": np.eye(128, dtype=np.float32),
        "c_jrow": (pos[:, None] + pos[None, :] - 128).astype(np.float32),
        "c_boff": np.tile(np.arange(NSEQ) * LTXT + 1, (128, 1)).astype(np.int32),
    }


def kernel(x, x_txt, L0_tok_proj_w, L0_tok_proj_b, L0_tok_pos_emb, L0_txt_emb, L0_attn_g1, L0_attn_b1,
           L0_attn_in_proj_w, L0_attn_conv_w, L0_attn_conv_b, L0_attn_x_proj_w, L0_attn_dt_proj_w, L0_attn_dt_proj_b,
           L0_attn_A_log, L0_attn_A_b_log, L0_attn_Dskip, L0_attn_out_proj_w, L0_attn_g2, L0_attn_b2, L0_attn_fc1_w,
           L0_attn_fc1_b, L0_attn_fc2_w, L0_attn_fc2_b, L0_ffn_weights_in, L0_ffn_weights_out):
    import concourse.bacc as bacc
    import numpy as np
    from concourse.bass_utils import run_bass_kernel_spmd

    def chunks(w, n):
        w = np.asarray(w)
        return w.reshape(n, w.shape[0] // n, *w.shape[1:]).swapaxes(0, 1)

    side = 128 // PATCH
    px = np.asarray(x).reshape(NSEQ, 2, side, PATCH, side, PATCH).transpose(0, 1, 2, 4, 3, 5)
    px = px.reshape(NSEQ * LIMG, FEAT).T
    ids = np.asarray(x_txt)
    xw = np.asarray(L0_attn_x_proj_w)
    xw = np.concatenate([xw[RANK:], xw[:RANK]])
    dtw = np.zeros((XD, INNER), np.float32)
    dtw[2 * STATE:] = np.asarray(L0_attn_dt_proj_w).T
    spread_a = lambda a: np.asarray(a).reshape(48, 8, STATE).transpose(2, 1, 0).reshape(128, 48)
    arrays = {
        "patches": chunks(px, FK), "w_tok": chunks(np.asarray(L0_tok_proj_w).T, FK),
        "pos": np.tile(np.asarray(L0_tok_pos_emb)[0], (PER, 1)),
        "tok_bias": np.tile(np.asarray(L0_tok_proj_b), (128, 1)),
        "x_pad": np.concatenate([np.full_like(ids, -1), ids], 1), "x_ids": ids.reshape(-1, 1),
        "emb": np.asarray(L0_txt_emb),
        "w_in": chunks(np.asarray(L0_attn_in_proj_w).T, 2), "w_x": chunks(xw.T, CH), "w_dt": dtw,
        "w_out": chunks(np.asarray(L0_attn_out_proj_w).T, CH), "w_fc1": chunks(np.asarray(L0_attn_fc1_w).T, 2),
        "w_fc2": chunks(np.asarray(L0_attn_fc2_w).T, CH), "w_fin": chunks(np.asarray(L0_ffn_weights_in).T, 2),
        "w_fout": np.asarray(L0_ffn_weights_out), "taps": chunks(L0_attn_conv_w, CH),
        "chan": np.stack([chunks(a, CH) for a in (L0_attn_conv_b, L0_attn_dt_proj_b, L0_attn_Dskip, L0_attn_fc1_b)], 1),
        "gains": np.stack([chunks(a, 2) for a in (L0_attn_g1, L0_attn_b1, L0_attn_g2, L0_attn_b2)], 1),
        "fc2_bias": np.tile(np.asarray(L0_attn_fc2_b), (128, 1)),
        "a_log": np.stack([spread_a(L0_attn_A_log), spread_a(L0_attn_A_b_log)], 1),
        **constants(),
    }
    nc = bacc.Bacc("TRN2", target_bir_lowering=False, num_devices=1)
    given, aps = {}, {}
    for name, a in arrays.items():
        given[f"in_{name}"] = a = np.ascontiguousarray(a)
        aps[name] = nc.dram_tensor(f"in_{name}", a.shape, mybir.dt.from_np(a.dtype), kind="ExternalInput").ap()
    out = nc.dram_tensor("out_0", (NSEQ, L, DIM), F32, kind="ExternalOutput").ap()
    build(nc, aps, out)
    r = run_bass_kernel_spmd(nc, [given], core_ids=[0])
    return r.results[0]["out_0"]
```

```python
from contextlib import ExitStack

import concourse.bass as bass
from concourse import mybir

F32 = mybir.dt.float32
BF16 = mybir.dt.bfloat16
I32 = mybir.dt.int32
ALU = mybir.AluOpType
ACT = mybir.ActivationFunctionType
AX = mybir.AxisListType

NSEQ, LIMG, LTXT = 16, 64, 128
L = LIMG + LTXT
DIM, INNER, STATE, RANK = 192, 384, 16, 12
HALF = DIM // 2
CH = INNER // 128
XD = 2 * STATE + RANK
PER = 2
COLS = PER * L
BLOCKS = NSEQ // PER
TILES = 3
PATCH = 16
FEAT = 2 * PATCH * PATCH
FK = FEAT // 128
TAPS = 4
UNITS = CH * 2 * 16
QUADS = UNITS // 4
NODES = 21
EPS = 1e-5
RING_W, RING_H, RING_A = 3, 12, 4
PRE_USES, POST_USES = 26, 15
MOVES = 12 * 16
XH, CONV_F, GATE, CONV_B, XPROJ_F, XPROJ_B, DT_F, REP_F, REP_B, DT_B = 0, 3, 6, 9, 12, 13, 14, 17, 19, 21
OUTP, NORM_T, FC1, FC2, FFF_T, LOGITS, COEF_T, FFF_OUT = 0, 2, 4, 7, 9, 11, 12, 13

PRE_AT = [(0, 2), (3, 2), (6, 2),
          (9, 4), (14, 4), (19, 4),
          (24, 2), (27, 2), (30, 2),
          (34, 4), (39, 4), (44, 4),
          (49, 3), (54, 3),
          (58, 1), (60, 1), (62, 1),
          (65, 1), (67, 1), (69, 1), (71, 1),
          (74, 1), (76, 1), (78, 1)]
PRE_TAKEN = {at + n: u for u, (at, n) in enumerate(PRE_AT)}
PRE1_AT = (81, 84)
SILU_AT = {33: (0, True), 50: (1, False)}
SOFT_EXP, SOFT_LN = (64, 80), (66, 82)
SOFT_V = ((67, 69, 70, 71), (83, 85, 86, 87))
SPLIT_HI, SPLIT_REST = ((71, 72), (87, 88)), ((73, 74), (89, 90))
SPLIT_MID, SPLIT_LO = ((74, 75), (90, 91)), ((76, 77), (92, 93))
POST_AT = [(12, 2), (18, 1), (28, 1), (31, 1), (36, 2), (39, 2), (42, 2), (57, 2), (61, 1), (70, 1), (73, 1),
           (77, 1), (84, 1), (88, 1), (91, 1)]
POST_TAKEN = {14: 0, 20: 1, 30: 2, 32: 3, 38: 4, 41: 5, 44: 6, 60: 7, 63: 8, 72: 9, 75: 10, 78: 11, 86: 12, 89: 13, 92: 14}
GELU_AT, WALK_AT = 54, 80
NORM0_AT, NORM1_AT = (21, 25), (64, 67)
LN_AT = (16, 24, 38)
TAKE_AT = {5: 2, 37: 0, 69: 1}


def build(nc, A, out):
    ctx = ExitStack()
    with ctx:
        def sb(name, shape, dt=F32):
            return ctx.enter_context(nc.sbuf_tensor(name, shape, dt))

        def sem(name):
            return ctx.enter_context(nc.semaphore(name))

        ident = sb("ident", [128, 128])
        sel_spread = sb("sel_spread", [96, 4, 128], BF16)
        sel_sum = sb("sel_sum", [128, 4, 32])
        sel_rep = sb("sel_rep", [XD, 2, 128])
        w_in = sb("w_in", [HALF, 2, 2 * INNER])
        w_x = sb("w_x", [128, CH, XD])
        w_dt = sb("w_dt", [XD, INNER])
        w_out = sb("w_out", [128, CH, DIM])
        w_fc1 = sb("w_fc1", [HALF, 2, INNER])
        w_fc2 = sb("w_fc2", [128, CH, DIM])
        w_fin = sb("w_fin", [HALF, 2, NODES])
        w_fout = sb("w_fout", [NODES, DIM])
        taps = sb("taps", [128, CH, TAPS])
        diag_tap = sb("diag_tap", [128, CH, TAPS, 128])
        diag_skip = sb("diag_skip", [128, CH, 128])
        chan = sb("chan", [128, 4, CH])
        gains = sb("gains", [HALF, 4, 2])
        fc2_bias = sb("fc2_bias", [128, DIM])
        a_log = sb("a_log", [128, 2, 48])
        mhalf = sb("mhalf", [128, TILES])
        h0 = sb("h0", [128, BLOCKS * TILES * DIM])
        nrm = sb("nrm", [128, TILES, DIM])
        x1T = sb("x1T", [HALF, 2, COLS])
        xh = sb("xh", [128, CH, COLS])
        t_e = sb("t_e", [128, CH, COLS])
        t_u = sb("t_u", [128, CH, COLS])
        t_l = sb("t_l", [128, CH, COLS])
        xc = sb("xc", [128, 2, 2, CH, COLS])
        gate = sb("gate", [128, 2, CH, COLS])
        xdbl = sb("xdbl", [XD, 2, COLS])
        parts = sb("parts", [128, 2, 3, CH * COLS], BF16)
        spread = sb("spread", [128, 2, 2, CH, 4 * COLS], BF16)
        rep = sb("rep", [128, 2, 2, 2, COLS])
        decay = sb("decay", [128, RING_A, COLS + 1])
        hring = sb("hring", [128, RING_H, COLS])
        yz = sb("yz", [128, CH, COLS])
        hh = sb("hh", [128, TILES, DIM])
        h1 = sb("h1", [128, TILES, DIM])
        pnrm = sb("pnrm", [128, TILES, DIM])
        pT = sb("pT", [HALF, 2, COLS])
        gl = sb("gl", [128, CH, COLS])
        st = sb("st", [128, TILES, 6])
        mean0 = sb("mean0", [128, BLOCKS * TILES])
        pad = sb("pad", [128, 1])
        rs0 = sb("rs0", [128, BLOCKS * TILES])
        mv1 = sb("mv1", [128, 2, TILES])
        ve = sb("ve", [128, TILES])
        rs1 = sb("rs1", [128, TILES])
        pst = sb("pst", [128, TILES, 6])
        pmv = sb("pmv", [128, 2, TILES])
        pve = sb("pve", [128, TILES])
        prs = sb("prs", [128, TILES])
        act_l = sb("act_l", [128, TILES, NODES])
        go_r = sb("go_r", [128, 2, TILES, NODES])
        go_l = sb("go_l", [128, 2, TILES, NODES])
        tree = sb("tree", [128, 2, TILES, NODES])
        tsum = sb("tsum", [128, 2, TILES])
        coefT = gl[0:NODES, 0, :]
        best = sb("best", [128, NSEQ])
        besti = sb("besti", [128, 2, NSEQ], I32)
        flag = sb("flag", [128, NSEQ])
        tok = sb("tok", [128, NSEQ], I32)
        boff = sb("boff", [128, NSEQ], I32)

        early = spread[:, :, :, :, :].rearrange("p a b c x -> p (a b c x)").bitcast(F32)
        shifted, plain, eq, run = (early[:, i * 2048:(i + 1) * 2048] for i in range(4))
        hflat = hring[:, :, :].rearrange("p a b -> p (a b)")
        patches = hflat[:, 0:FK * 1024].rearrange("p (k t) -> p k t", k=FK)
        pflat = parts[:, :, :, :].rearrange("p a b c -> p (a b c)").bitcast(F32)
        w_tok = pflat[:, 0:FK * DIM].rearrange("p (k d) -> p k d", k=FK)
        pos = pflat[:, 768:768 + DIM]
        tok_bias = pflat[:, 960:960 + DIM]
        jrow = pflat[:, 1152:1152 + LTXT]

        ps = ctx.enter_context(nc.psum_tensor("ps", [128, 8, 512], F32))
        DT = [ps[:, i, 0:COLS] for i in (0, 1)]
        BU = [ps[:, i, 0:COLS] for i in (2, 3, 4)]
        Y, PRE, POST = (ps[:, i, 0:COLS] for i in (5, 6, 7))

        S = {n: sem(n) for n in (
            "txt_loaded", "img_loaded", "w_loaded", "best_ready", "keyT_ready", "rosa_idx", "ids_lo",
            "ids_hi", "emb_lo", "emb_hi", "text_masked", "img_ready", "img_taken", "img_done", "consts_set",
            "key_ready", "exp_a", "a_ready", "diag_ready", "pro",
            "dt_filled", "bu_filled", "decay_ready", "bu_ready", "state_ready", "prod_ready", "reduced",
            "y_taken", "pre_full", "pre_free", "post_full", "post_free",
            "ln0_ve", "ln0_rs", "ln1_ve", "ln1_rs", "x1_ready", "pre_v",
            "soft_e", "soft_l", "dt_ready", "hi_ready", "rest_ready", "mid_ready", "lo_ready",
            "hh_ve", "hh_rs", "m_ready", "h1_ve", "h1_rs", "v_ready", "post_v", "act_ready", "coef_ready",
            "soft_v", "hh_u", "mean_kept", "hh_b", "h1_sum", "tree_v", "sent_f_dt", "sent_f_dtu", "sent_b_dt", "sent_b_dtu",
            "out_sent", "silu_done", "gelu_done")}
        SENT = (("sent_f_dt", "sent_f_dtu"), ("sent_b_dt", "sent_b_dtu"))

        def at_least(eng, name, k, per, more):
            if isinstance(k, int) and k * per + more <= 0:
                return
            eng.wait_ge(S[name], k * per + more)

        def tile(k, t):
            return h0[:, bass.ds((k * TILES + t) * DIM, DIM)]

        def cols_of(a, t):
            if t < PER:
                return a[:, t * L + LIMG:(t + 1) * L]
            return a.rearrange("p (b l) -> p b l", b=PER)[:, :, 0:LIMG]

        def unit(n):
            return n // 32, n // 16 % 2, n % 16 // 4, n % 4

        sel_raw = t_u[0:96, :, :].rearrange("p c x -> p (c x)")[:, 0:4 * 128]
        WLOADS = [(sel_raw, "c_spread"), (sel_sum[:, :, :], "c_sum"), (sel_rep[:, :, :], "c_rep"),
                  (w_in[:, :, :], "w_in"), (w_x[:, :, :], "w_x"), (w_dt[:, :], "w_dt"), (w_out[:, :, :], "w_out"),
                  (w_fc1[:, :, :], "w_fc1"), (w_fc2[:, :, :], "w_fc2"), (w_fin[:, :, :], "w_fin"),
                  (w_fout[:, :], "w_fout"), (taps[:, :, :], "taps"), (chan[:, :, :], "chan"),
                  (gains[:, :, :], "gains"), (fc2_bias[:, :], "fc2_bias"), (a_log[:, :, :], "a_log")]

        block = ctx.enter_context(nc.Block())

        @block.sync
        def _(sp):
            xpad = A["x_pad"]
            sp.dma_start(shifted.rearrange("p (b i) -> p b i", b=NSEQ).bitcast(I32),
                         bass.AP(xpad.tensor, 0, [[1, 128], [2 * LTXT, NSEQ], [1, LTXT]])).then_inc(S["txt_loaded"], 16)
            sp.dma_start(plain.rearrange("p (b i) -> p b i", b=NSEQ).bitcast(I32),
                         bass.AP(xpad.tensor, LTXT, [[0, 128], [2 * LTXT, NSEQ], [1, LTXT]])).then_inc(S["txt_loaded"], 16)
            sp.dma_start(jrow, A["c_jrow"]).then_inc(S["txt_loaded"], 16)
            sp.dma_start(ident[:, :], A["c_ident"]).then_inc(S["txt_loaded"], 16)
            sp.dma_start(boff[:, :], A["c_boff"]).then_inc(S["txt_loaded"], 16)
            sp.dma_start(w_tok, A["w_tok"]).then_inc(S["img_loaded"], 16)
            sp.dma_start(pos, A["pos"]).then_inc(S["img_loaded"], 16)
            sp.dma_start(tok_bias, A["tok_bias"]).then_inc(S["img_loaded"], 16)
            sp.dma_start(patches, A["patches"]).then_inc(S["img_loaded"], 16)
            for dst, name in WLOADS:
                sp.dma_start(dst, A[name]).then_inc(S["w_loaded"], 16)

            def send_parts(kk, dr, i):
                at_least(sp, "lo_ready", kk, 4, 2 * dr + i + 1)
                at_least(sp, "bu_filled", kk, UNITS, -16 * (1 - dr))
                v = parts[:, i, :, :].rearrange("p s (c x) -> p s c x", c=CH)
                for s in range(3):
                    for q in range(4):
                        sp.dma_start(spread[32 * s:32 * s + 32, i, dr, :, q * COLS:(q + 1) * COLS],
                                     v[32 * q:32 * q + 32, s, :, :]).then_inc(S[SENT[dr][i]], 16)

            def store(kk):
                at_least(sp, "post_free", kk, POST_USES, POST_USES)
                for b in range(PER):
                    sp.dma_start(out[bass.ds(kk * PER + b, 1), LIMG:L, :].rearrange("b l d -> (b l) d"),
                                 h1[:, b, :]).then_inc(S["out_sent"], 16)
                    sp.dma_start(out[bass.ds(kk * PER + b, 1), 0:LIMG, :].rearrange("b l d -> (b l) d"),
                                 h1[b * LIMG:(b + 1) * LIMG, 2, :]).then_inc(S["out_sent"], 16)

            for dr in range(2):
                for i in range(2):
                    send_parts(0, dr, i)

            def body(k, pre, post):
                if pre:
                    for dr in range(2):
                        for i in range(2):
                            send_parts(k + 1, dr, i)
                if post:
                    store(k - 1)

            body(0, True, False)
            with sp.Fori(0, 2) as it:
                body(it * 2 + 1, True, True)
                body(it * 2 + 2, True, True)
            body(5, True, True)
            body(6, True, True)
            body(7, False, True)
            store(7)
            sp.wait_ge(S["out_sent"], BLOCKS * 64)

        @block.gpsimd
        def _(pool):
            g = nc.gpsimd
            g.memset(mhalf[:, :], -0.5).then_inc(S["consts_set"], 1)
            pool.wait_ge(S["rosa_idx"], 1)
            for b in range(NSEQ):
                g.indirect_dma_start(tok[:, b:b + 1], None, A["x_ids"],
                                     bass.IndirectOffsetOnAxis(besti[:, 1, b:b + 1], 0))\
                    .then_inc(S["ids_lo" if b < PER else "ids_hi"], 16)
            for b in range(NSEQ):
                if b == 0:
                    pool.wait_ge(S["ids_lo"], 16 * PER)
                if b == PER:
                    pool.wait_ge(S["ids_hi"], 16 * (NSEQ - PER))
                t = b // PER * TILES + b % PER
                g.indirect_dma_start(h0[:, t * DIM:(t + 1) * DIM], None, A["emb"],
                                     bass.IndirectOffsetOnAxis(tok[:, b:b + 1], 0))\
                    .then_inc(S["emb_lo" if b < PER else "emb_hi"], 16)

            def power(var, res, kk, ready, done, per=1):
                at_least(pool, ready, kk, 1, 1)
                g.tensor_tensor(res, var, mhalf[:, :], ALU.pow).then_inc(S[done], 1)

            def pre1(kk, step):
                if step == 0:
                    power(ve[:, :], rs0[:, bass.ds(kk * TILES, TILES)], kk, "ln0_ve", "ln0_rs")
                else:
                    power(ve[:, :], rs1[:, :], kk, "ln1_ve", "ln1_rs")

            def prod(k, par, n):
                c, dr, j, q = unit(n)
                at_least(pool, "state_ready", k, UNITS, n + 1)
                h = hring[:, n % RING_H, :]
                g.tensor_tensor(h, h, rep[:, par, dr, 1, :], ALU.mult).then_inc(S["prod_ready"], 1)

            def body(k, par, pre2, pre1_, post):
                for n in range(UNITS):
                    prod(k, par, n)
                    if pre1_ and n in LN_AT[:2]:
                        pre1(k + 2, LN_AT.index(n))
                    if post and n == NORM0_AT[0]:
                        power(pve[:, :], prs[:, :], k - 1, "hh_ve", "hh_rs")
                    if post and n == NORM1_AT[0]:
                        power(pve[:, :], prs[:, :], k - 1, "h1_ve", "h1_rs")

            pool.wait_ge(S["consts_set"], 1)
            pre1(0, 0)
            pre1(0, 1)
            pre1(1, 0)
            pre1(1, 1)
            body(0, 0, True, True, False)
            with pool.Fori(0, 2) as it:
                body(it * 2 + 1, 1, True, True, True)
                body(it * 2 + 2, 0, True, True, True)
            body(5, 1, True, True, True)
            body(6, 0, True, False, True)
            body(7, 1, False, False, True)
            power(pve[:, :], prs[:, :], 7, "hh_ve", "hh_rs")
            power(pve[:, :], prs[:, :], 7, "h1_ve", "h1_rs")

        @block.scalar
        def _(act):
            a = nc.scalar.activation
            act.wait_ge(S["exp_a"], 1)
            a(a_log[:, :, :], a_log[:, :, :], ACT.Exp).then_inc(S["a_ready"], 1)

            def full(name, kk, per, i):
                at_least(act, name, kk, per, i + 1)

            def pre1(kk, half):
                full("pre_full", kk, PRE_USES, half)
                a(x1T[:, half, :], PRE[0:HALF, :], ACT.Identity, scale=gains[:, 0, half:half + 1],
                  bias=gains[:, 1, half:half + 1]).then_inc(S["pre_free"], 1)

            def pre2(kk, par, u):
                full("pre_full", kk, PRE_USES, 2 + u)
                if u < CONV_F:
                    if u == 0:
                        at_least(act, "lo_ready", kk, 4, 0)
                    a(xh[:, u, :], PRE, ACT.Identity).then_inc(S["pre_free"], 1)
                elif u < GATE or CONV_B <= u < XPROJ_F:
                    dr, c = (0, u - CONV_F) if u < GATE else (1, u - CONV_B)
                    if c == 0 and dr == 0:
                        at_least(act, "reduced", kk, QUADS, -QUADS)
                    a(xc[:, par, dr, c, :], PRE, ACT.Identity, bias=chan[:, 0, c:c + 1]).then_inc(S["pre_free"], 1)
                elif u < CONV_B:
                    c = u - GATE
                    if c == 0:
                        at_least(act, "y_taken", kk, CH, -CH)
                    a(gate[:, par, c, :], PRE, ACT.Identity).then_inc(S["pre_free"], 1)
                elif u < DT_F:
                    a(xdbl[:, u - XPROJ_F, :], PRE[0:XD, :], ACT.Identity).then_inc(S["pre_free"], 1)
                elif u < REP_F or u >= DT_B:
                    dr, c = (0, u - DT_F) if u < REP_F else (1, u - DT_B)
                    if c == 0:
                        at_least(act, "rest_ready", kk, 4, 2 * dr)
                    a(xh[:, c, :], PRE, ACT.Relu, bias=chan[:, 1, c:c + 1])
                    a(t_e[:, c, :], PRE, ACT.Abs, bias=chan[:, 1, c:c + 1]).then_inc(S["pre_free"], 1)
                else:
                    dr, which = divmod(u - REP_F, 2)
                    if u == REP_F:
                        at_least(act, "prod_ready", kk, UNITS, -UNITS)
                    a(rep[:, par, dr, which, :], PRE, ACT.Identity).then_inc(S["pre_free"], 1)

            def silu(kk, par, dr, with_gate):
                at_least(act, "pre_free", kk, PRE_USES, 2 + (CONV_B if dr == 0 else XPROJ_F))
                if with_gate:
                    a(gate[:, par, :, :], gate[:, par, :, :], ACT.Silu)
                a(xc[:, par, dr, :, :], xc[:, par, dr, :, :], ACT.Silu).then_inc(S["silu_done"], 1)

            def soft_exp(kk, dr):
                at_least(act, "pre_free", kk, PRE_USES, 2 + CH + (DT_F, DT_B)[dr])
                a(t_e[:, :, :], t_e[:, :, :], ACT.Exp, scale=-1.0).then_inc(S["soft_e"], 1)

            def soft_ln(kk, dr):
                at_least(act, "soft_e", kk, 2, dr + 1)
                at_least(act, "lo_ready", kk, 4, 2 * dr)
                a(t_u[:, :, :], t_e[:, :, :], ACT.Identity, bias=1.0)
                a(t_l[:, :, :], t_e[:, :, :], ACT.Ln, bias=1.0).then_inc(S["soft_l"], 1)

            def split_hi(kk, dr, i):
                at_least(act, "dt_ready", kk, 4, 2 * dr + i + 1)
                at_least(act, SENT[1 - dr][i], kk, MOVES, (dr - 1) * MOVES + dr * MOVES)
                a(parts[:, i, 0, :], (xh, t_e)[i][:, :, :].rearrange("p c x -> p (c x)"), ACT.Identity)\
                    .then_inc(S["hi_ready"], 1)

            def split_mid(kk, dr, i):
                at_least(act, "rest_ready", kk, 4, 2 * dr + i + 1)
                a(parts[:, i, 1, :], (t_u, t_l)[i][:, :, :].rearrange("p c x -> p (c x)"), ACT.Identity)\
                    .then_inc(S["mid_ready"], 1)

            def gelu(kk):
                at_least(act, "post_free", kk, POST_USES, FC2)
                a(gl[:, :, :], gl[:, :, :], ACT.Gelu).then_inc(S["gelu_done"], 1)

            def post(kk, u):
                if u in (NORM_T, NORM_T + 1):
                    full("post_full", kk, POST_USES, u)
                    half = u - NORM_T
                    a(pT[:, half, :], POST[0:HALF, :], ACT.Identity, scale=gains[:, 2, half:half + 1],
                      bias=gains[:, 3, half:half + 1]).then_inc(S["post_free"], 1)
                elif FC1 <= u < FC2:
                    full("post_full", kk, POST_USES, u)
                    c = u - FC1
                    a(gl[:, c, :], POST, ACT.Identity, bias=chan[:, 3, c:c + 1]).then_inc(S["post_free"], 1)
                elif u in (FFF_T, FFF_T + 1):
                    full("post_full", kk, POST_USES, u)
                    a(pT[:, u - FFF_T, :], POST[0:HALF, :], ACT.Identity).then_inc(S["post_free"], 1)
                elif u == LOGITS:
                    full("post_full", kk, POST_USES, u)
                    a(act_l[:, :, :].rearrange("p t n -> p (t n)"), POST[:, 0:TILES * NODES], ACT.Gelu)\
                        .then_inc(S["act_ready"], 1)
                elif u == COEF_T:
                    full("post_full", kk, POST_USES, u)
                    a(coefT, POST[0:NODES, :], ACT.Identity).then_inc(S["post_free"], 1)

            def decay_of(k, n):
                c, dr, j, q = unit(n)
                at_least(act, "dt_filled", k, UNITS, n + 1)
                at_least(act, "state_ready", k, UNITS, n - RING_A + 1)
                g = c * 16 + q * 4 + j
                lo = 1 if dr == 0 else 0
                src = DT[n % 2].rearrange("p (b l) -> p b l", b=PER)[:, :, lo:lo + L - 1]
                dst = decay[:, n % RING_A, 1:COLS + 1].rearrange("p (b l) -> p b l", b=PER)[:, :, 0:L - 1]
                a(dst, src, ACT.Exp, scale=a_log[:, dr, g:g + 1]).then_inc(S["decay_ready"], 1)

            def body(k, par, pre, pre1_, post_):
                for n in range(UNITS):
                    decay_of(k, n)
                    if pre:
                        if n in PRE_TAKEN:
                            pre2(k + 1, 1 - par, PRE_TAKEN[n])
                        if n in SILU_AT:
                            silu(k + 1, 1 - par, *SILU_AT[n])
                        for dr in range(2):
                            if n == SOFT_EXP[dr]:
                                soft_exp(k + 1, dr)
                            if n == SOFT_LN[dr]:
                                soft_ln(k + 1, dr)
                            if n in SPLIT_HI[dr]:
                                split_hi(k + 1, dr, SPLIT_HI[dr].index(n))
                            if n in SPLIT_MID[dr]:
                                split_mid(k + 1, dr, SPLIT_MID[dr].index(n))
                    if pre1_ and n - 2 in PRE1_AT:
                        pre1(k + 2, PRE1_AT.index(n - 2))
                    if post_ and n in POST_TAKEN:
                        post(k - 1, POST_TAKEN[n])
                    if post_ and n == GELU_AT:
                        gelu(k - 1)

            act.wait_ge(S["diag_ready"], 1)
            act.wait_ge(S["w_loaded"], 16 * len(WLOADS))
            pre1(0, 0)
            pre1(0, 1)
            for u in range(24):
                pre2(0, 0, u)
                if u in (CONV_B - 1, XPROJ_F - 1):
                    silu(0, 0, int(u > CONV_B), u < CONV_B)
                if u in (REP_F - 1, PRE_USES - 3):
                    dr = int(u > REP_F)
                    soft_exp(0, dr)
                    soft_ln(0, dr)
                    for i in range(2):
                        split_hi(0, dr, i)
                    for i in range(2):
                        split_mid(0, dr, i)
            pre1(1, 0)
            pre1(1, 1)
            body(0, 0, True, True, False)
            with act.Fori(0, 2) as it:
                body(it * 2 + 1, 1, True, True, True)
                body(it * 2 + 2, 0, True, True, True)
            body(5, 1, True, True, True)
            body(6, 0, True, False, True)
            body(7, 1, False, False, True)
            for u in range(POST_USES):
                post(7, u)
                if u == FC2 - 1:
                    gelu(7)

        @block.tensor
        def _(pe):
            mm = nc.tensor.matmul

            def pre_bank(kk, i):
                at_least(pe, "pre_free", kk, PRE_USES, i)

            def post_bank(kk, i):
                at_least(pe, "post_free", kk, POST_USES, i)

            def turn(bank, src, half, full):
                for t in range(TILES):
                    i = nc.tensor.transpose(cols_of(bank[0:HALF, :], t), src[:, t, half * HALF:(half + 1) * HALF],
                                            ident[:, :])
                i.then_inc(S[full], 1)

            def pre1(kk, half):
                if half == 0:
                    at_least(pe, "x1_ready", kk, 1, 1)
                pre_bank(kk, half)
                turn(PRE, nrm, half, "pre_full")

            def conv(dr, c, s):
                o, i = (slice(s, L), slice(0, L - s)) if dr == 0 else (slice(0, L - s), slice(s, L))
                return mm(PRE.rearrange("p (b l) -> p b l", b=PER)[:, :, o], diag_tap[:, c, TAPS - 1 - s, :],
                          xh[:, c, :].rearrange("p (b l) -> p b l", b=PER)[:, :, i],
                          start=(s == 0), stop=(s == TAPS - 1))

            def pre2(kk, par, u, s):
                steps = PRE_AT[u][1]
                if s == 0:
                    pre_bank(kk, 2 + u)
                if u < CONV_F or GATE <= u < CONV_B:
                    e = u if u < CONV_F else CH + u - GATE
                    last = mm(PRE, w_in[:, s, e * 128:(e + 1) * 128], x1T[:, s, :], start=(s == 0), stop=(s == 1))
                elif u < GATE:
                    last = conv(0, u - CONV_F, s)
                elif u < XPROJ_F:
                    last = conv(1, u - CONV_B, s)
                elif u < DT_F:
                    dr = u - XPROJ_F
                    if s == 0:
                        at_least(pe, "silu_done", kk, 2, dr + 1)
                    last = mm(PRE[0:XD, :], w_x[:, s, :], xc[:, par, dr, s, :], start=(s == 0), stop=(s == CH - 1))
                elif u < REP_F or u >= DT_B:
                    dr, c = (0, u - DT_F) if u < REP_F else (1, u - DT_B)
                    last = mm(PRE, w_dt[:, c * 128:(c + 1) * 128], xdbl[:, dr, :], start=True, stop=True)
                else:
                    dr, which = divmod(u - REP_F, 2)
                    last = mm(PRE, sel_rep[:, which, :], xdbl[:, dr, :], start=True, stop=True)
                if s == steps - 1:
                    last.then_inc(S["pre_full"], 1)

            def by_token(col, width, t, terms):
                for b in range(1 if t < PER else PER):
                    rows, at = (slice(0, 128), t * L + LIMG) if t < PER else (slice(b * LIMG, (b + 1) * LIMG), b * L)
                    for i, (x, w) in enumerate(terms):
                        last = mm(ps[rows, 7, col:col + width], x[:, at:at + rows.stop - rows.start], w,
                                  start=(i == 0), stop=(i == len(terms) - 1), tile_position=(0, rows.start))
                return last

            def tokens(src, w, s, t):
                return by_token(s * DIM, DIM, t, [(src[:, c, :], w[:, c, :]) for c in range(CH)])

            def post(kk, u, s):
                if u in (OUTP, OUTP + 1):
                    if s == 0:
                        at_least(pe, "y_taken", kk, CH, CH)
                        post_bank(kk, u)
                    last = tokens(yz, w_out, s, s if u == OUTP else 2)
                    if s == POST_AT[u][1] - 1:
                        last.then_inc(S["post_full"], 1)
                elif u in (NORM_T, NORM_T + 1):
                    at_least(pe, "m_ready", kk, 1, 1)
                    post_bank(kk, u)
                    turn(POST, pnrm, u - NORM_T, "post_full")
                elif FC1 <= u < FC2:
                    if s == 0:
                        post_bank(kk, u)
                    c = u - FC1
                    last = mm(POST, w_fc1[:, s, c * 128:(c + 1) * 128], pT[:, s, :], start=(s == 0), stop=(s == 1))
                    if s == 1:
                        last.then_inc(S["post_full"], 1)
                elif u in (FC2, FC2 + 1):
                    if s == 0:
                        at_least(pe, "gelu_done", kk, 1, 1)
                        post_bank(kk, u)
                    last = tokens(gl, w_fc2, s, s if u == FC2 else 2)
                    if s == POST_AT[u][1] - 1:
                        last.then_inc(S["post_full"], 1)
                elif u in (FFF_T, FFF_T + 1):
                    at_least(pe, "v_ready", kk, 1, 1)
                    post_bank(kk, u)
                    turn(POST, pnrm, u - FFF_T, "post_full")
                elif u == LOGITS:
                    post_bank(kk, u)
                    for t in range(TILES):
                        last = by_token(t * NODES, NODES, t, [(pT[:, i, :], w_fin[:, i, :]) for i in range(2)])
                    last.then_inc(S["post_full"], 1)
                elif u == COEF_T:
                    at_least(pe, "coef_ready", kk, 1, 1)
                    post_bank(kk, u)
                    for t in range(TILES):
                        last = nc.tensor.transpose(ps[0:NODES, 7, t * 128:(t + 1) * 128], tree[:, 1, t, :], ident[:, :])
                    last.then_inc(S["post_full"], 1)
                else:
                    post_bank(kk, u)
                    for o, t in enumerate((0, 1) if u == FFF_OUT else (2,)):
                        last = mm(ps[:, 7, o * DIM:(o + 1) * DIM], coefT[:, t * 128:(t + 1) * 128], w_fout[:, :],
                                  start=True, stop=True)
                    last.then_inc(S["post_full"], 1)

            def spread_of(k, n):
                c, dr, j, q = unit(n)
                if n in (0, 16):
                    for i in range(2):
                        at_least(pe, SENT[dr][i], k, MOVES, MOVES)
                at_least(pe, "decay_ready", k, UNITS, n - 1)
                mm(DT[n % 2], sel_spread[:, j, :], spread[0:96, 0, dr, c, q * COLS:(q + 1) * COLS],
                   start=True, stop=True).then_inc(S["dt_filled"], 1)
                at_least(pe, "bu_ready", k, UNITS, n - RING_W + 1)
                mm(BU[n % RING_W], sel_spread[:, j, :], spread[0:96, 1, dr, c, q * COLS:(q + 1) * COLS],
                   start=True, stop=True).then_inc(S["bu_filled"], 1)

            def reduce(k, par, quad):
                c, dr, j, _ = unit(4 * quad)
                if quad % 8 == 0:
                    at_least(pe, "y_taken", k, CH, c)
                    for d in range(2):
                        mm(Y, diag_skip[:, c, :], xc[:, par, d, c, :], start=(d == 0), stop=False)
                at_least(pe, "prod_ready", k, UNITS, 4 * quad + 4)
                for q in range(4):
                    last = mm(ps[32 * q:32 * q + 32, 5, 0:COLS], sel_sum[:, j, :], hring[:, (4 * quad + q) % RING_H, :],
                              start=False, stop=(quad % 8 == 7), tile_position=(0, 32 * q))
                last.then_inc(S["reduced"], 1)

            def body(k, par, pre, pre1_, post_):
                for n in range(UNITS):
                    spread_of(k, n)
                    if n % 4 == 1:
                        q = n // 4
                        if q >= 2:
                            reduce(k, par, q - 2)
                        elif not (isinstance(k, int) and k == 0):
                            reduce(k - 1, 1 - par, QUADS - 2 + q)
                    if pre:
                        for u, (at, steps) in enumerate(PRE_AT):
                            if at <= n < at + steps:
                                pre2(k + 1, 1 - par, u, n - at)
                    if pre1_ and n in PRE1_AT:
                        pre1(k + 2, PRE1_AT.index(n))
                    if post_:
                        for u, (at, steps) in enumerate(POST_AT):
                            if at <= n < at + steps:
                                post(k - 1, u, n - at)

            pe.wait_ge(S["txt_loaded"], 5 * 16)
            pe.wait_ge(S["key_ready"], 1)
            for b in range(NSEQ):
                last = nc.tensor.transpose(ps[:, b // 4, b % 4 * 128:(b % 4 + 1) * 128], run[:, b * 128:(b + 1) * 128],
                                           ident[:, :])
            last.then_inc(S["keyT_ready"], 1)
            pe.wait_ge(S["img_loaded"], 4 * 16)
            for k in range(BLOCKS):
                if k >= 2:
                    pe.wait_ge(S["img_taken"], k - 1)
                for f in range(FK):
                    last = mm(ps[:, 4 + k % 2, 0:DIM], patches[:, f, k * 128:(k + 1) * 128], w_tok[:, f, :],
                              start=(f == 0), stop=(f == FK - 1))
                last.then_inc(S["img_ready"], 1)
            pe.wait_ge(S["w_loaded"], 16 * len(WLOADS))
            pe.wait_ge(S["diag_ready"], 1)
            pre1(0, 0)
            pre1(0, 1)
            for u in range(24):
                for s in range(PRE_AT[u][1]):
                    pre2(0, 0, u, s)
            pre1(1, 0)
            pre1(1, 1)
            pe.wait_ge(S["img_taken"], BLOCKS)
            body(0, 0, True, True, False)
            with pe.Fori(0, 2) as it:
                body(it * 2 + 1, 1, True, True, True)
                body(it * 2 + 2, 0, True, True, True)
            body(5, 1, True, True, True)
            body(6, 0, True, False, True)
            body(7, 1, False, False, True)
            reduce(7, 1, QUADS - 2)
            reduce(7, 1, QUADS - 1)
            for u in range(POST_USES):
                for s in range(POST_AT[u][1]):
                    post(7, u, s)

        @block.vector
        def _(dve):
            v = nc.vector

            class Steps:

                def __init__(self, name, per):
                    self.name, self.per, self.n = name, per, 0

                def done(self, ins, kk):
                    self.n += 1
                    ins.then_inc(S[self.name], 1)
                    dve.wait_ge(S[self.name], kk * self.per + self.n)

            once = Steps("pro", 0)
            v.memset(decay[:, :, :], 0.0)
            v.memset(tree[:, :, :, :], 0.0)
            dve.wait_ge(S["txt_loaded"], 5 * 16)
            once.done(v.tensor_tensor(eq, shifted.bitcast(I32), plain.bitcast(I32), ALU.is_equal), 0)
            once.done(v.memset(shifted, 1.0), 0)
            once.done(v.tensor_tensor_scan(run, shifted, eq, 0.0, ALU.add, ALU.mult), 0)
            js = jrow.rearrange("p (o i) -> p o i", o=1).broadcast_to([128, NSEQ, LTXT])
            as3 = lambda x: x.rearrange("p (b i) -> p b i", b=NSEQ)
            once.done(v.scalar_tensor_tensor(as3(shifted), as3(run), 128.0, js, ALU.mult, ALU.add), 0)
            v.tensor_tensor(run, shifted, eq, ALU.mult).then_inc(S["key_ready"], 1)
            dve.wait_ge(S["w_loaded"], 16 * len(WLOADS))
            v.tensor_scalar(a_log[:, :, :], a_log[:, :, :], 80.0, None, ALU.min).then_inc(S["exp_a"], 1)
            v.tensor_copy(sel_spread[:, :, :].rearrange("p j m -> p (j m)"), sel_raw)
            for c in range(CH):
                for k in range(TAPS):
                    v.tensor_scalar(diag_tap[:, c, k, :], ident[:, :], taps[:, c, k:k + 1], None, ALU.mult)
                v.tensor_scalar(diag_skip[:, c, :], ident[:, :], chan[:, 2, c:c + 1], None, ALU.mult)
            dve.wait_ge(S["a_ready"], 1)
            v.tensor_scalar(a_log[:, :, :], a_log[:, :, :], -1.0, None, ALU.mult).then_inc(S["diag_ready"], 1)
            dve.wait_ge(S["keyT_ready"], 1)
            once.done(v.tensor_reduce(best[:, :], ps[:, 0:4, :].rearrange("p a (b j) -> p (a b) j", j=128), AX.X,
                                      ALU.max), 0)
            v.tensor_scalar(flag[:, :], best[:, :], 128.0, None, ALU.is_ge)
            once.done(v.tensor_copy(besti[:, 0, :], best[:, :]), 0)
            once.done(v.tensor_scalar(besti[:, 0, :], besti[:, 0, :], 127, None, ALU.bitwise_and), 0)
            v.tensor_tensor(besti[:, 1, :], besti[:, 0, :], boff[:, :], ALU.add).then_inc(S["rosa_idx"], 1)
            dve.wait_ge(S["img_loaded"], 4 * 16)
            once.done(v.tensor_tensor(pos, pos, tok_bias, ALU.add), 0)
            for k in range(BLOCKS):
                dve.wait_ge(S["img_ready"], k + 1)
                v.tensor_tensor(tile(k, 2), ps[:, 4 + k % 2, 0:DIM], pos, ALU.add).then_inc(S["img_taken"], 1)
            dve.wait_ge(S["img_taken"], BLOCKS)

            def mask_text(b0, b1):
                for b in range(b0, b1):
                    x = tile(b // PER, b % PER)
                    last = v.tensor_scalar(x, x, flag[:, b:b + 1], None, ALU.mult)
                last.then_inc(S["text_masked"], 1)

            PRE_V = 5

            def after(sem_name, value):
                dve.wait_ge(S[sem_name], value)
                v.memset(pad[:, :], 0.0)

            def pre1(kk, step):
                if step == 0:
                    for t in range(TILES):
                        last = v.bn_stats(st[:, t, :], tile(kk, t))
                    last.then_inc(S["pre_v"], 1)
                    after("pre_v", kk * PRE_V + 1)
                    for t in range(TILES):
                        last = v.bn_aggr(mv1[:, :, t], st[:, t, :])
                    last.then_inc(S["pre_v"], 1)
                    dve.wait_ge(S["pre_v"], kk * PRE_V + 2)
                    v.tensor_copy(mean0[:, bass.ds(kk * TILES, TILES)], mv1[:, 0, :]).then_inc(S["mean_kept"], 1)
                    v.tensor_scalar(ve[:, :], mv1[:, 1, :], EPS, None, ALU.add).then_inc(S["ln0_ve"], 1)
                elif step == 1:
                    at_least(dve, "ln0_rs", kk, 1, 1)
                    at_least(dve, "mean_kept", kk, 1, 1)
                    at_least(dve, "pre_full", kk, PRE_USES, -PRE_USES + 2)
                    for t in range(TILES):
                        last = v.tensor_scalar(nrm[:, t, :], tile(kk, t), mean0[:, bass.ds(kk * TILES + t, 1)],
                                               rs0[:, bass.ds(kk * TILES + t, 1)], ALU.subtract, ALU.mult)
                    last.then_inc(S["pre_v"], 1)
                    dve.wait_ge(S["pre_v"], kk * PRE_V + 3)
                    for t in range(TILES):
                        last = v.bn_stats(st[:, t, :], nrm[:, t, :])
                    last.then_inc(S["pre_v"], 1)
                    after("pre_v", kk * PRE_V + 4)
                    for t in range(TILES):
                        last = v.bn_aggr(mv1[:, :, t], st[:, t, :])
                    last.then_inc(S["pre_v"], 1)
                    dve.wait_ge(S["pre_v"], kk * PRE_V + 5)
                    v.tensor_scalar(ve[:, :], mv1[:, 1, :], EPS, None, ALU.add).then_inc(S["ln1_ve"], 1)
                else:
                    at_least(dve, "ln1_rs", kk, 1, 1)
                    for t in range(TILES):
                        last = v.tensor_scalar(nrm[:, t, :], nrm[:, t, :], mv1[:, 0, t:t + 1], rs1[:, t:t + 1],
                                               ALU.subtract, ALU.mult)
                    last.then_inc(S["x1_ready"], 1)

            def flat(x):
                return x[:, :, :].rearrange("p c x -> p (c x)")

            def soft(kk, par, dr, step):
                base = kk * 4 + 2 * dr
                if step == 0:
                    at_least(dve, "soft_l", kk, 2, dr + 1)
                    v.scalar_tensor_tensor(flat(t_u), flat(t_u), -1.0, flat(t_e), ALU.add, ALU.subtract)\
                        .then_inc(S["soft_v"], 1)
                elif step == 1:
                    dve.wait_ge(S["soft_v"], base + 1)
                    v.tensor_tensor(flat(t_l), flat(t_l), flat(t_u), ALU.subtract).then_inc(S["soft_v"], 1)
                elif step == 2:
                    dve.wait_ge(S["soft_v"], base + 2)
                    v.tensor_tensor(flat(xh), flat(xh), flat(t_l), ALU.add).then_inc(S["dt_ready"], 1)
                else:
                    dve.wait_ge(S["dt_ready"], base + 1)
                    v.tensor_tensor(flat(t_e), flat(xh), xc[:, par, dr, :, :].rearrange("p c x -> p (c x)"), ALU.mult)\
                        .then_inc(S["dt_ready"], 1)

            def rest(kk, dr, i):
                at_least(dve, "hi_ready", kk, 4, 2 * dr + i + 1)
                v.tensor_tensor(flat((t_u, t_l)[i]), flat((xh, t_e)[i]), parts[:, i, 0, :], ALU.subtract)\
                    .then_inc(S["rest_ready"], 1)

            def low(kk, dr, i):
                at_least(dve, "mid_ready", kk, 4, 2 * dr + i + 1)
                v.tensor_tensor(parts[:, i, 2, :], flat((t_u, t_l)[i]), parts[:, i, 1, :], ALU.subtract)\
                    .then_inc(S["lo_ready"], 1)

            def take_y(k, par, c):
                at_least(dve, "reduced", k, QUADS, 8 * c + 8)
                if c == 0:
                    at_least(dve, "post_full", k, POST_USES, OUTP + 2 - POST_USES)
                v.tensor_tensor(yz[:, c, :], Y, gate[:, par, c, :], ALU.mult).then_inc(S["y_taken"], 1)

            POST_V = 5

            def two(x, u, first):
                return x[:, 0:2, :] if u == first else x[:, 2:3, :]

            def bank(u, first):
                n = 2 if u == first else 1
                return ps[:, 7, 0:n * DIM].rearrange("p (t d) -> p t d", d=DIM)

            def post(kk, u):
                if u in (OUTP, OUTP + 1):
                    at_least(dve, "post_full", kk, POST_USES, u + 1)
                    tiles = (0, 1) if u == OUTP else (2,)
                    for t in tiles:
                        last = v.tensor_scalar(hh[:, t, :], tile(kk, t), mean0[:, bass.ds(kk * TILES + t, 1)],
                                               rs0[:, bass.ds(kk * TILES + t, 1)], ALU.subtract, ALU.mult)
                    last.then_inc(S["hh_u"], 1)
                    dve.wait_ge(S["hh_u"], kk * 2 + u + 1)
                    x = two(hh, u, OUTP)
                    v.tensor_tensor(x, bank(u, OUTP), x, ALU.add).then_inc(S["post_free"], 1)
                elif u in (FC2, FC2 + 1):
                    at_least(dve, "post_full", kk, POST_USES, u + 1)
                    at_least(dve, "out_sent", kk, 64, 0)
                    x = two(h1, u, FC2)
                    v.tensor_tensor(x, bank(u, FC2), two(hh, u, FC2), ALU.add).then_inc(S["post_free"], 1)
                    dve.wait_ge(S["post_free"], kk * POST_USES + u + 1)
                    n = 2 if u == FC2 else 1
                    t = 0 if u == FC2 else 2
                    v.tensor_tensor(x, x, h0[:, bass.ds((kk * TILES + t) * DIM, n * DIM)]
                                    .rearrange("p (t d) -> p t d", d=DIM), ALU.add).then_inc(S["h1_sum"], 1)
                elif u in (FFF_OUT, FFF_OUT + 1):
                    at_least(dve, "post_full", kk, POST_USES, u + 1)
                    x = two(h1, u, FFF_OUT)
                    v.tensor_tensor(x, bank(u, FFF_OUT), x, ALU.add).then_inc(S["post_free"], 1)

            def post_norm(kk, which, part):
                src = (hh, h1)[which]
                base = kk * 4 + 2 * which
                if part == 0:
                    if which == 0:
                        at_least(dve, "post_free", kk, POST_USES, OUTP + 2)
                    else:
                        at_least(dve, "h1_sum", kk, 2, 2)
                    for t in range(TILES):
                        last = v.bn_stats(pst[:, t, :], src[:, t, :])
                    last.then_inc(S["post_v"], 1)
                    after("post_v", base + 1)
                    for t in range(TILES):
                        last = v.bn_aggr(pmv[:, :, t], pst[:, t, :])
                    last.then_inc(S["post_v"], 1)
                    dve.wait_ge(S["post_v"], base + 2)
                    v.tensor_scalar(pve[:, :], pmv[:, 1, :], EPS, None, ALU.add)\
                        .then_inc(S[("hh_ve", "h1_ve")[which]], 1)
                else:
                    at_least(dve, ("hh_rs", "h1_rs")[which], kk, 1, 1)
                    for t in range(TILES):
                        last = v.tensor_scalar(pnrm[:, t, :], src[:, t, :], pmv[:, 0, t:t + 1], prs[:, t:t + 1],
                                               ALU.subtract, ALU.mult)
                    last.then_inc(S[("m_ready", "v_ready")[which]], 1)
                    if which == 0:
                        dve.wait_ge(S["m_ready"], kk + 1)
                        v.tensor_tensor(hh[:, :, :], hh[:, :, :], fc2_bias[:, :].rearrange("p (o d) -> p o d", o=1)
                                        .broadcast_to([128, TILES, DIM]), ALU.add).then_inc(S["hh_b"], 1)
                        dve.wait_ge(S["hh_b"], kk + 1)

            TREE_V = 11

            def walk(kk):
                s = Steps("tree_v", TREE_V)
                reached, coef = tree[:, 0, :, :], tree[:, 1, :, :]
                at_least(dve, "act_ready", kk, 1, 1)
                v.tensor_scalar(go_r[:, 0, :, :], ps[:, 7, 0:TILES * NODES].rearrange("p (t n) -> p t n", n=NODES),
                                0.0, None, ALU.is_gt).then_inc(S["post_free"], 1)
                dve.wait_ge(S["post_free"], kk * POST_USES + LOGITS + 1)
                s.done(v.tensor_scalar(go_l[:, 0, :, :], go_r[:, 0, :, :], -1.0, 1.0, ALU.mult, ALU.add), kk)
                v.tensor_tensor(go_r[:, 1, :, :], go_r[:, 0, :, :], act_l[:, :, :], ALU.mult)
                s.done(v.tensor_tensor(go_l[:, 1, :, :], go_l[:, 0, :, :], act_l[:, :, :], ALU.mult), kk)
                v.tensor_copy(tree[:, :, :, 1:2], go_l[:, :, :, 0:1])
                s.done(v.tensor_copy(tree[:, :, :, 2:3], go_r[:, :, :, 0:1]), kk)

                def level(n0, n1):
                    m = tree[:, 0:1, :, n0:n1].broadcast_to([128, 2, TILES, n1 - n0])
                    for off, go in ((1, go_l), (2, go_r)):
                        last = v.tensor_tensor(tree[:, :, :, 2 * n0 + off:2 * n1 + off - 1:2], m, go[:, :, :, n0:n1],
                                               ALU.mult)
                    s.done(last, kk)

                level(1, 3)
                level(3, 7)
                level(7, 10)
                s.done(v.tensor_reduce(tsum[:, 0, :], reached[:, :, 10:15], AX.X, ALU.add), kk)
                s.done(v.tensor_tensor(reached[:, :, 20], reached[:, :, 20], tsum[:, 0, :], ALU.add), kk)
                s.done(v.tensor_tensor(go_r[:, 0, :, 10:21], reached[:, :, 10:21], act_l[:, :, 10:21], ALU.mult), kk)
                s.done(v.tensor_reduce(tsum[:, 1, :], go_r[:, 0, :, 10:21], AX.X, ALU.add), kk)
                s.done(v.tensor_tensor(coef[:, :, 20], coef[:, :, 20], tsum[:, 1, :], ALU.add), kk)
                v.scalar_tensor_tensor(coef[:, :, 20], act_l[:, :, 20], 5.0, coef[:, :, 20], ALU.mult, ALU.add)\
                    .then_inc(S["coef_ready"], 1)
                assert s.n == TREE_V, s.n

            def times_b(k, par, n):
                c, dr, j, q = unit(n)
                at_least(dve, "bu_filled", k, UNITS, n + 1)
                if n in (0, 16):
                    at_least(dve, "pre_free", k, PRE_USES, 2 + REP_F + 2 * dr + 2)
                if n % 4 == 0:
                    at_least(dve, "reduced", k, QUADS, n // 4 - 2)
                v.tensor_tensor(hring[:, n % RING_H, :], BU[n % RING_W], rep[:, par, dr, 0, :], ALU.mult)\
                    .then_inc(S["bu_ready"], 1)

            def scan(k, n):
                c, dr, j, q = unit(n)
                at_least(dve, "decay_ready", k, UNITS, n + 1)
                at_least(dve, "bu_ready", k, UNITS, n + 1)
                way = slice(None, None, 1 if dr == 0 else -1)
                h = hring[:, n % RING_H, :][:, way]
                v.tensor_tensor_scan(h, decay[:, n % RING_A, dr:dr + COLS][:, way], h, 0.0, ALU.mult, ALU.add)\
                    .then_inc(S["state_ready"], 1)

            def body(k, par, pre, pre1_, post_):
                for n in range(UNITS):
                    times_b(k, par, n)
                    if n:
                        scan(k, n - 1)
                    elif not (isinstance(k, int) and k == 0):
                        scan(k - 1, UNITS - 1)
                    if n in TAKE_AT:
                        c = TAKE_AT[n]
                        if c < CH - 1:
                            take_y(k, par, c)
                        elif not (isinstance(k, int) and k == 0):
                            take_y(k - 1, 1 - par, c)
                    if pre:
                        for dr in range(2):
                            if n in SOFT_V[dr]:
                                soft(k + 1, 1 - par, dr, SOFT_V[dr].index(n))
                            if n in SPLIT_REST[dr]:
                                rest(k + 1, dr, SPLIT_REST[dr].index(n))
                            if n in SPLIT_LO[dr]:
                                low(k + 1, dr, SPLIT_LO[dr].index(n))
                    if pre1_ and n in LN_AT:
                        pre1(k + 2, LN_AT.index(n))
                    if post_:
                        if n in POST_TAKEN:
                            post(k - 1, POST_TAKEN[n])
                        for which, at in enumerate((NORM0_AT, NORM1_AT)):
                            if n in at:
                                post_norm(k - 1, which, at.index(n))
                        if n == WALK_AT:
                            walk(k - 1)

            dve.wait_ge(S["emb_lo"], 16 * PER)
            mask_text(0, PER)
            dve.wait_ge(S["text_masked"], 1)
            for step in range(3):
                pre1(0, step)
            dve.wait_ge(S["emb_hi"], 16 * (NSEQ - PER))
            mask_text(PER, NSEQ)
            dve.wait_ge(S["text_masked"], 2)
            for dr in range(2):
                for step in range(4):
                    soft(0, 0, dr, step)
                for i in range(2):
                    rest(0, dr, i)
                for i in range(2):
                    low(0, dr, i)
            for step in range(3):
                pre1(1, step)
            body(0, 0, True, True, False)
            with dve.Fori(0, 2) as it:
                body(it * 2 + 1, 1, True, True, True)
                body(it * 2 + 2, 0, True, True, True)
            body(5, 1, True, True, True)
            body(6, 0, True, False, True)
            body(7, 1, False, False, True)
            scan(7, UNITS - 1)
            take_y(7, 1, CH - 1)
            post(7, OUTP)
            post(7, OUTP + 1)
            post_norm(7, 0, 0)
            post_norm(7, 0, 1)
            post(7, FC2)
            post(7, FC2 + 1)
            post_norm(7, 1, 0)
            post_norm(7, 1, 1)
            walk(7)
            post(7, FFF_OUT)
            post(7, FFF_OUT + 1)


def constants():
    import numpy as np

    spread = np.zeros((3, 32, 4, STATE, 8), np.float32)
    total = np.zeros((STATE, 8, 4, 32), np.float32)
    for j in range(4):
        for d in range(8):
            spread[:, 8 * j + d, j, :, d] = 1
            total[:, d, j, 8 * j + d] = 1
    rep = np.zeros((XD, 2, STATE, 8), np.float32)
    for n in range(STATE):
        rep[n, 0, n, :] = 1
        rep[STATE + n, 1, n, :] = 1
    pos = np.arange(LTXT)
    return {
        "c_spread": spread.reshape(96, 4 * 128), "c_sum": total.reshape(128, 4, 32),
        "c_rep": rep.reshape(XD, 2, 128), "c_ident": np.eye(128, dtype=np.float32),
        "c_jrow": (pos[:, None] + pos[None, :] - 128).astype(np.float32),
        "c_boff": np.tile(np.arange(NSEQ) * LTXT + 1, (128, 1)).astype(np.int32),
    }


def kernel(x, x_txt, L0_tok_proj_w, L0_tok_proj_b, L0_tok_pos_emb, L0_txt_emb, L0_attn_g1, L0_attn_b1,
           L0_attn_in_proj_w, L0_attn_conv_w, L0_attn_conv_b, L0_attn_x_proj_w, L0_attn_dt_proj_w, L0_attn_dt_proj_b,
           L0_attn_A_log, L0_attn_A_b_log, L0_attn_Dskip, L0_attn_out_proj_w, L0_attn_g2, L0_attn_b2, L0_attn_fc1_w,
           L0_attn_fc1_b, L0_attn_fc2_w, L0_attn_fc2_b, L0_ffn_weights_in, L0_ffn_weights_out):
    import concourse.bacc as bacc
    import numpy as np
    from concourse.bass_utils import run_bass_kernel_spmd

    def chunks(w, n):
        w = np.asarray(w)
        return w.reshape(n, w.shape[0] // n, *w.shape[1:]).swapaxes(0, 1)

    side = 128 // PATCH
    px = np.asarray(x).reshape(NSEQ, 2, side, PATCH, side, PATCH).transpose(0, 1, 2, 4, 3, 5)
    px = px.reshape(NSEQ * LIMG, FEAT).T
    ids = np.asarray(x_txt)
    xw = np.asarray(L0_attn_x_proj_w)
    xw = np.concatenate([xw[RANK:], xw[:RANK]])
    dtw = np.zeros((XD, INNER), np.float32)
    dtw[2 * STATE:] = np.asarray(L0_attn_dt_proj_w).T
    spread_a = lambda a: np.asarray(a).reshape(48, 8, STATE).transpose(2, 1, 0).reshape(128, 48)
    arrays = {
        "patches": chunks(px, FK), "w_tok": chunks(np.asarray(L0_tok_proj_w).T, FK),
        "pos": np.tile(np.asarray(L0_tok_pos_emb)[0], (PER, 1)),
        "tok_bias": np.tile(np.asarray(L0_tok_proj_b), (128, 1)),
        "x_pad": np.concatenate([np.full_like(ids, -1), ids], 1), "x_ids": ids.reshape(-1, 1),
        "emb": np.asarray(L0_txt_emb),
        "w_in": chunks(np.asarray(L0_attn_in_proj_w).T, 2), "w_x": chunks(xw.T, CH), "w_dt": dtw,
        "w_out": chunks(np.asarray(L0_attn_out_proj_w).T, CH), "w_fc1": chunks(np.asarray(L0_attn_fc1_w).T, 2),
        "w_fc2": chunks(np.asarray(L0_attn_fc2_w).T, CH), "w_fin": chunks(np.asarray(L0_ffn_weights_in).T, 2),
        "w_fout": np.asarray(L0_ffn_weights_out), "taps": chunks(L0_attn_conv_w, CH),
        "chan": np.stack([chunks(a, CH) for a in (L0_attn_conv_b, L0_attn_dt_proj_b, L0_attn_Dskip, L0_attn_fc1_b)], 1),
        "gains": np.stack([chunks(a, 2) for a in (L0_attn_g1, L0_attn_b1, L0_attn_g2, L0_attn_b2)], 1),
        "fc2_bias": np.tile(np.asarray(L0_attn_fc2_b), (128, 1)),
        "a_log": np.stack([spread_a(L0_attn_A_log), spread_a(L0_attn_A_b_log)], 1),
        **constants(),
    }
    nc = bacc.Bacc("TRN2", target_bir_lowering=False, num_devices=1)
    given, aps = {}, {}
    for name, a in arrays.items():
        given[f"in_{name}"] = a = np.ascontiguousarray(a)
        aps[name] = nc.dram_tensor(f"in_{name}", a.shape, mybir.dt.from_np(a.dtype), kind="ExternalInput").ap()
    out = nc.dram_tensor("out_0", (NSEQ, L, DIM), F32, kind="ExternalOutput").ap()
    build(nc, aps, out)
    r = run_bass_kernel_spmd(nc, [given], core_ids=[0])
    return r.results[0]["out_0"]
```

```python
from contextlib import ExitStack

import concourse.bass as bass
from concourse import mybir

F32 = mybir.dt.float32
BF16 = mybir.dt.bfloat16
I32 = mybir.dt.int32
ALU = mybir.AluOpType
ACT = mybir.ActivationFunctionType
AX = mybir.AxisListType

NSEQ, LIMG, LTXT = 16, 64, 128
L = LIMG + LTXT
DIM, INNER, STATE, RANK = 192, 384, 16, 12
HALF = DIM // 2
CH = INNER // 128
XD = 2 * STATE + RANK
PER = 2
COLS = PER * L
BLOCKS = NSEQ // PER
TILES = 3
PATCH = 16
FEAT = 2 * PATCH * PATCH
FK = FEAT // 128
TAPS = 4
UNITS = CH * 2 * 16
PAIRS = UNITS // 2
QUADS = UNITS // 4
NODES = 21
EPS = 1e-5
RING_D, RING_W, RING_H, RING_A = 3, 2, 12, 8
SKEW = 2
PRE_USES, POST_USES = 20, 15
MOVES = 12 * 16
CONV_STEPS = 2 * (TAPS - 1)
CONVS = CH * CONV_STEPS
MARGIN = TAPS - 1
GATE, PRE1, XPROJ, DT_F, XH, REP_F, DT_B, REP_B = (0, 1, 2), (3, 6), (4, 5), (7, 8, 9), (10, 13, 17), (11, 12), \
    (14, 15, 16), (18, 19)
SECOND = PRE1 + XH
PROLOGUE = [(u, 0) for u in (*PRE1, *XH, *GATE, *XPROJ, *DT_F, *DT_B, *REP_F)] + \
    [(u, 1) for u in (*PRE1, XH[0])] + [(u, 0) for u in REP_B] + [(u, 1) for u in XH[1:]]
OUTP, NORM_T, FC1, FC2, FFF_T, LOGITS, COEF_T, FFF_OUT = 0, 2, 4, 7, 9, 11, 12, 13

PRE_AT = [(7, 2), (11, 2), (15, 2),
          (19, 1), (24, 3), (29, 3), (34, 1),
          (38, 1), (42, 1), (46, 1),
          (50, 2), (54, 1), (58, 1), (63, 2),
          (68, 1), (72, 1), (76, 1),
          (80, 2), (85, 1), (89, 1)]
PRE_TAKEN = {a: u for u, a in enumerate((10, 14, 18, 20, 28, 33, 36, 40, 44, 48, 53, 56, 60, 66, 70, 74, 78, 83, 87, 91))}
CONV_AT = [51, 53, 55, 56, 58, 59, 65, 67, 69, 71, 73, 75, 81, 83, 85, 87, 89, 91]
SILU_AT = 19
REDUCE_AT = 1
SOFT_EXP, SOFT_LN = (49, 79), (51, 81)
SOFT_V = ((52, 54, 56, 58), (82, 83, 84, 86))
SPLIT_HI, SPLIT_REST = ((62, 64), (88, 90)), ((63, 65), (88, 90))
SPLIT_MID, SPLIT_LO = ((68, 70), (92, 94)), ((73, 76), (93, 95))
POST_AT = [(9, 2), (14, 1), (23, 1), (26, 1), (29, 2), (33, 2), (37, 2), (44, 2), (48, 1), (57, 1), (60, 1),
           (64, 1), (71, 1), (74, 1), (78, 1)]
POST_TAKEN = {a: u for u, a in enumerate((11, 15, 25, 28, 32, 36, 40, 46, 49, 59, 62, 66, 73, 75, 79))}
GELU_AT, WALK_AT = 41, 67
NORM0_AT, NORM1_AT = (16, 21), (50, 55)
LN_AT = (6, 10, 15)
TAKE_AT = {5: 2, 37: 0, 69: 1}


def build(nc, A, out):
    ctx = ExitStack()
    with ctx:
        def sb(name, shape, dt=F32):
            return ctx.enter_context(nc.sbuf_tensor(name, shape, dt))

        def sem(name):
            return ctx.enter_context(nc.semaphore(name))

        ident = sb("ident", [128, 128])
        sel_spread = sb("sel_spread", [128, 4, 128], BF16)
        sel_sum = sb("sel_sum", [128, 4, 32])
        sel_rep = sb("sel_rep", [XD, 2, 128])
        w_in = sb("w_in", [HALF, 2, 2 * INNER])
        w_x = sb("w_x", [128, CH, XD])
        w_dt = sb("w_dt", [XD, INNER])
        w_out = sb("w_out", [128, CH, DIM])
        w_fc1 = sb("w_fc1", [HALF, 2, INNER])
        w_fc2 = sb("w_fc2", [128, CH, DIM])
        w_fin = sb("w_fin", [HALF, 2, NODES])
        w_fout = sb("w_fout", [NODES, DIM])
        taps = sb("taps", [128, CH, TAPS])
        diag_skip = sb("diag_skip", [128, CH, 128])
        chan = sb("chan", [128, 4, CH])
        gains = sb("gains", [HALF, 4, 2])
        fc2_bias = sb("fc2_bias", [128, DIM])
        a_log = sb("a_log", [128, 2, 48])
        mhalf = sb("mhalf", [128, TILES])
        h0 = sb("h0", [128, BLOCKS * TILES * DIM])
        nrm = sb("nrm", [128, TILES, DIM])
        x1T = sb("x1T", [HALF, 2, COLS])
        xh = sb("xh", [128, CH, COLS])
        t_e = sb("t_e", [128, CH, COLS])
        t_u = sb("t_u", [128, CH, COLS])
        t_l = sb("t_l", [128, CH, COLS])
        prods = sb("prods", [128, TAPS, 2 * MARGIN + PER * (L + MARGIN)])
        xc = sb("xc", [128, 2, 2, CH, COLS])
        gate = sb("gate", [128, 2, CH, COLS])
        xdbl = sb("xdbl", [XD, 2, COLS])
        parts = sb("parts", [128, 2, 3, CH * COLS], BF16)
        spread = sb("spread", [128, 2, 2, CH, 4 * COLS], BF16)
        rep = sb("rep", [128, 2, 2, 2, COLS])
        decay = sb("decay", [128, RING_A // 2, 2 * COLS + 1])
        hring = sb("hring", [128, RING_H, COLS])
        yz = sb("yz", [128, CH, COLS])
        hh = sb("hh", [128, TILES, DIM])
        h1 = sb("h1", [128, TILES, DIM])
        pnrm = yz[:, 1:CH, :].rearrange("p c x -> p (c x)")[:, 0:TILES * DIM].rearrange("p (t d) -> p t d", d=DIM)
        pT = sb("pT", [HALF, 2, COLS])
        gl = prods[:, 0:CH, MARGIN:MARGIN + PER * (L + MARGIN)]
        gl4 = gl.rearrange("p c (b l) -> p c b l", b=PER)[:, :, :, 0:L]
        st = sb("st", [128, TILES, 6])
        mean0 = sb("mean0", [128, BLOCKS * TILES])
        pad = sb("pad", [128, 1])
        rs0 = sb("rs0", [128, BLOCKS * TILES])
        mv1 = sb("mv1", [128, 2, TILES])
        ve = sb("ve", [128, TILES])
        rs1 = sb("rs1", [128, TILES])
        pst = sb("pst", [128, TILES, 6])
        pmv = sb("pmv", [128, 2, TILES])
        pve = sb("pve", [128, TILES])
        prs = sb("prs", [128, TILES])
        act_l = sb("act_l", [128, TILES, NODES])
        go_r = sb("go_r", [128, 2, TILES, NODES])
        go_l = sb("go_l", [128, 2, TILES, NODES])
        tree = sb("tree", [128, 2, TILES, NODES])
        tsum = sb("tsum", [128, 2, TILES])
        coefT = pT[0:NODES, 0, :]
        FIRST = 2 * PER
        best = sb("best", [128, NSEQ])
        besti = sb("besti", [128, 2, NSEQ], I32)
        flag = sb("flag", [128, NSEQ])
        tok = sb("tok", [128, NSEQ], I32)
        boff = sb("boff", [128, NSEQ], I32)

        early = spread[:, :, :, :, :].rearrange("p a b c x -> p (a b c x)").bitcast(F32)
        shifted, plain, eq, run = (early[:, i * 2048:(i + 1) * 2048] for i in range(4))
        hflat = hring[:, :, :].rearrange("p a b -> p (a b)")
        patches = hflat[:, 0:FK * 1024].rearrange("p (k t) -> p k t", k=FK)
        pflat = parts[:, :, :, :].rearrange("p a b c -> p (a b c)").bitcast(F32)
        w_tok = pflat[:, 0:FK * DIM].rearrange("p (k d) -> p k d", k=FK)
        pos = pflat[:, 768:768 + DIM]
        tok_bias = pflat[:, 960:960 + DIM]
        jrow = pflat[:, 1152:1152 + LTXT]

        ps = ctx.enter_context(nc.psum_tensor("ps", [128, 8, 512], F32))
        DT = [ps[:, i, 0:COLS] for i in range(RING_D)]
        BU = [ps[:, RING_D + i, 0:COLS] for i in range(RING_W)]
        Y, PRE, POST = (ps[:, i, 0:COLS] for i in (5, 6, 7))

        S = {n: sem(n) for n in (
            "txt_loaded", "img_loaded", "w_loaded", "best_ready", "keyT_ready", "rosa_idx", "ids_lo",
            "ids_hi", "emb_lo", "emb_hi", "text_masked", "img_ready", "img_taken", "img_done", "consts_set",
            "key_ready", "exp_a", "a_ready", "diag_ready", "pro",
            "dt_filled", "bu_filled", "decay_ready", "bu_ready", "state_ready", "prod_ready", "reduced",
            "y_taken", "pre_full", "pre_free", "post_full", "post_free",
            "ln0_ve", "ln0_rs", "ln1_ve", "ln1_rs", "x1_ready", "pre_v",
            "soft_e", "soft_l", "dt_ready", "hi_ready", "rest_ready", "mid_ready", "lo_ready",
            "hh_ve", "hh_rs", "m_ready", "h1_ve", "h1_rs", "v_ready", "post_v", "act_ready", "coef_ready",
            "soft_v", "hh_u", "mean_kept", "hh_b", "h1_sum", "tree_v", "sent_f_dt", "sent_f_dtu", "sent_b_dt", "sent_b_dtu",
            "out_sent", "silu_done", "gelu_done", "rows_zeroed", "conv_ready")}
        SENT = (("sent_f_dt", "sent_f_dtu"), ("sent_b_dt", "sent_b_dtu"))

        def at_least(eng, name, k, per, more):
            if isinstance(k, int) and k * per + more <= 0:
                return
            eng.wait_ge(S[name], k * per + more)

        def pre_use(k, u, kk=None):
            if k is None:
                return 0, PRE_USES, PROLOGUE.index((u, kk)) + 1
            before = [x for x in range(u) if not (isinstance(k, int) and k == BLOCKS - 2 and x in SECOND)]
            return k, PRE_USES, len(PROLOGUE) + len(before) + 1

        def pre_bank(k, u, kk):
            return POST if k is None and PROLOGUE.index((u, kk)) % 2 else PRE

        def tile(k, t):
            return h0[:, bass.ds((k * TILES + t) * DIM, DIM)]

        def conv(eng, k, kk, par, i):
            c, s, dr = i // CONV_STEPS, i % CONV_STEPS // 2 + 1, i % 2
            dst = xc[:, par, dr, c, :].rearrange("p (b l) -> p b l", b=PER)
            off = MARGIN + (s if dr else -s)
            moved = prods[:, s, off:off + PER * (L + MARGIN)].rearrange("p (b l) -> p b l", b=PER)[:, :, 0:L]
            if s == 1:
                at_least(eng, "pre_free", *pre_use(k, XH[c], kk))
                at_least(eng, "reduced", kk, QUADS, -2 * QUADS + 8 * c + 1)
                first = prods[:, 0, MARGIN:MARGIN + PER * (L + MARGIN)].rearrange("p (b l) -> p b l", b=PER)
                last = eng.tensor_tensor(dst, first[:, :, 0:L], moved, ALU.add)
            else:
                at_least(eng, "conv_ready", kk, CONVS, i - 1)
                last = eng.tensor_tensor(dst, dst, moved, ALU.add)
            last.then_inc(S["conv_ready"], 1)

        def soft_buffers(kk, dr):
            if dr and isinstance(kk, int) and kk == 0:
                return [hring[:, CH * i:CH * i + CH, :] for i in range(4)]
            return [x[:, :, :] for x in (xh, t_e, t_u, t_l)]

        def cols_of(a, t):
            if t < PER:
                return a[:, t * L + LIMG:(t + 1) * L]
            return a.rearrange("p (b l) -> p b l", b=PER)[:, :, 0:LIMG]

        def unit(n):
            return n // 32, n // 16 % 2, n % 16 // 4, n % 4

        sel_raw = t_u[:, :, :].rearrange("p c x -> p (c x)")[:, 0:4 * 128]
        WLOADS = [(sel_raw, "c_spread"), (sel_sum[:, :, :], "c_sum"), (sel_rep[:, :, :], "c_rep"),
                  (w_in[:, :, :], "w_in"), (w_x[:, :, :], "w_x"), (w_dt[:, :], "w_dt"), (w_out[:, :, :], "w_out"),
                  (w_fc1[:, :, :], "w_fc1"), (w_fc2[:, :, :], "w_fc2"), (w_fin[:, :, :], "w_fin"),
                  (w_fout[:, :], "w_fout"), (taps[:, :, :], "taps"), (chan[:, :, :], "chan"),
                  (gains[:, :, :], "gains"), (fc2_bias[:, :], "fc2_bias"), (a_log[:, :, :], "a_log")]

        block = ctx.enter_context(nc.Block())

        @block.sync
        def _(sp):
            xpad = A["x_pad"]
            sp.dma_start(shifted.rearrange("p (b i) -> p b i", b=NSEQ).bitcast(I32),
                         bass.AP(xpad.tensor, 0, [[1, 128], [2 * LTXT, NSEQ], [1, LTXT]])).then_inc(S["txt_loaded"], 16)
            sp.dma_start(plain.rearrange("p (b i) -> p b i", b=NSEQ).bitcast(I32),
                         bass.AP(xpad.tensor, LTXT, [[0, 128], [2 * LTXT, NSEQ], [1, LTXT]])).then_inc(S["txt_loaded"], 16)
            sp.dma_start(jrow, A["c_jrow"]).then_inc(S["txt_loaded"], 16)
            sp.dma_start(ident[:, :], A["c_ident"]).then_inc(S["txt_loaded"], 16)
            sp.dma_start(boff[:, :], A["c_boff"]).then_inc(S["txt_loaded"], 16)
            sp.dma_start(w_tok, A["w_tok"]).then_inc(S["img_loaded"], 16)
            sp.dma_start(pos, A["pos"]).then_inc(S["img_loaded"], 16)
            sp.dma_start(tok_bias, A["tok_bias"]).then_inc(S["img_loaded"], 16)
            sp.dma_start(patches, A["patches"]).then_inc(S["img_loaded"], 16)
            for dst, name in WLOADS:
                sp.dma_start(dst, A[name]).then_inc(S["w_loaded"], 16)

            def send_parts(kk, dr, i):
                at_least(sp, "lo_ready", kk, 4, 2 * dr + i + 1)
                at_least(sp, "bu_filled", kk, UNITS, -16 * (1 - dr))
                v = parts[:, i, :, :].rearrange("p s (c x) -> p s c x", c=CH)
                for s in range(3):
                    for q in range(4):
                        sp.dma_start(spread[32 * s:32 * s + 32, i, dr, :, q * COLS:(q + 1) * COLS],
                                     v[32 * q:32 * q + 32, s, :, :]).then_inc(S[SENT[dr][i]], 16)

            def store(kk):
                at_least(sp, "post_free", kk, POST_USES, POST_USES)
                for b in range(PER):
                    sp.dma_start(out[bass.ds(kk * PER + b, 1), LIMG:L, :].rearrange("b l d -> (b l) d"),
                                 h1[:, b, :]).then_inc(S["out_sent"], 16)
                    sp.dma_start(out[bass.ds(kk * PER + b, 1), 0:LIMG, :].rearrange("b l d -> (b l) d"),
                                 h1[b * LIMG:(b + 1) * LIMG, 2, :]).then_inc(S["out_sent"], 16)

            for dr in range(2):
                for i in range(2):
                    send_parts(0, dr, i)

            def body(k, pre, post):
                if pre:
                    for dr in range(2):
                        for i in range(2):
                            send_parts(k + 1, dr, i)
                if post:
                    store(k - 1)

            body(0, True, False)
            with sp.Fori(0, 2) as it:
                body(it * 2 + 1, True, True)
                body(it * 2 + 2, True, True)
            body(5, True, True)
            body(6, True, True)
            body(7, False, True)
            store(7)
            sp.wait_ge(S["out_sent"], BLOCKS * 64)

        @block.gpsimd
        def _(pool):
            g = nc.gpsimd
            g.memset(mhalf[:, :], -0.5).then_inc(S["consts_set"], 1)
            pool.wait_ge(S["rosa_idx"], 1)
            def ids(b):
                g.indirect_dma_start(tok[:, b:b + 1], None, A["x_ids"],
                                     bass.IndirectOffsetOnAxis(besti[:, 1, b:b + 1], 0))\
                    .then_inc(S["ids_lo" if b < FIRST else "ids_hi"], 16)

            def rows(b):
                t = b // PER * TILES + b % PER
                g.indirect_dma_start(h0[:, t * DIM:(t + 1) * DIM], None, A["emb"],
                                     bass.IndirectOffsetOnAxis(tok[:, b:b + 1], 0))\
                    .then_inc(S["emb_lo" if b < FIRST else "emb_hi"], 16)

            for b in range(FIRST):
                ids(b)
            pool.wait_ge(S["ids_lo"], 16 * FIRST)
            for b in range(FIRST):
                rows(b)

            def power(var, res, kk, ready, done, per=1):
                at_least(pool, ready, kk, 1, 1)
                g.tensor_tensor(res, var, mhalf[:, :], ALU.pow).then_inc(S[done], 1)

            def pre1(kk, step):
                if step == 0:
                    power(ve[:, :], rs0[:, bass.ds(kk * TILES, TILES)], kk, "ln0_ve", "ln0_rs")
                else:
                    power(ve[:, :], rs1[:, :], kk, "ln1_ve", "ln1_rs")

            def prod(k, par, pair):
                n = 2 * pair
                c, dr, j, q = unit(n)
                at_least(pool, "state_ready", k, PAIRS, pair + 1)
                h = hring[:, n % RING_H:n % RING_H + 2, :]
                C = rep[:, par, dr, 1:2, :].broadcast_to([128, 2, COLS])
                g.tensor_tensor(h, h, C, ALU.mult).then_inc(S["prod_ready"], 1)

            def body(k, par, pre2, pre1_, post):
                for n in range(UNITS):
                    if n % 2:
                        prod(k, par, n // 2)
                    if pre1_ and n in CONV_AT:
                        conv(pool, k, k + 2, par, CONV_AT.index(n))
                    if pre1_ and n in LN_AT[:2]:
                        pre1(k + 2, LN_AT.index(n))
                    if post and n == NORM0_AT[0]:
                        power(pve[:, :], prs[:, :], k - 1, "hh_ve", "hh_rs")
                    if post and n == NORM1_AT[0]:
                        power(pve[:, :], prs[:, :], k - 1, "h1_ve", "h1_rs")

            pool.wait_ge(S["consts_set"], 1)
            for kk in range(2):
                pre1(kk, 0)
                pre1(kk, 1)
            for b in range(FIRST, NSEQ):
                ids(b)
            pool.wait_ge(S["keyT_ready"], 1)
            pool.wait_ge(S["ln1_rs"], 2)
            g.memset(spread[96:128, :, :, :, :], 0.0).then_inc(S["rows_zeroed"], 1)
            pool.wait_ge(S["rows_zeroed"], 1)
            pool.wait_ge(S["ids_hi"], 16 * (NSEQ - FIRST))
            for b in range(FIRST, NSEQ):
                rows(b)
            for i in range(CONVS):
                conv(pool, None, 1, 1, i)
            body(0, 0, True, True, False)
            with pool.Fori(0, 2) as it:
                body(it * 2 + 1, 1, True, True, True)
                body(it * 2 + 2, 0, True, True, True)
            body(5, 1, True, True, True)
            body(6, 0, True, False, True)
            body(7, 1, False, False, True)
            power(pve[:, :], prs[:, :], 7, "hh_ve", "hh_rs")
            power(pve[:, :], prs[:, :], 7, "h1_ve", "h1_rs")

        @block.scalar
        def _(act):
            a = nc.scalar.activation
            act.wait_ge(S["exp_a"], 1)
            a(a_log[:, :, :], a_log[:, :, :], ACT.Exp).then_inc(S["a_ready"], 1)

            def full(name, kk, per, i):
                at_least(act, name, kk, per, i + 1)

            def pre(k, kk, par, u):
                at_least(act, "pre_full", *pre_use(k, u, kk))
                bank = pre_bank(k, u, kk)
                if u in PRE1:
                    half = PRE1.index(u)
                    a(x1T[:, half, :], bank[0:HALF, :], ACT.Identity, scale=gains[:, 0, half:half + 1],
                      bias=gains[:, 1, half:half + 1]).then_inc(S["pre_free"], 1)
                elif u in XH:
                    c = XH.index(u)
                    at_least(act, "conv_ready", kk, CONVS, c * CONV_STEPS)
                    if k is not None and c == 0:
                        at_least(act, "post_full", k, POST_USES, FC2 + 2 - POST_USES)
                    for s in range(TAPS):
                        dst = prods[:, s, MARGIN:MARGIN + PER * (L + MARGIN)].rearrange("p (b l) -> p b l", b=PER)
                        last = a(dst[:, :, 0:L], bank.rearrange("p (b l) -> p b l", b=PER), ACT.Identity,
                                 scale=taps[:, c, TAPS - 1 - s:TAPS - s], bias=chan[:, 0, c:c + 1] if s == 0 else 0.0)
                    last.then_inc(S["pre_free"], 1)
                elif u in GATE:
                    c = GATE.index(u)
                    if c == 0:
                        at_least(act, "y_taken", kk, CH, -CH)
                    a(gate[:, par, c, :], bank, ACT.Identity).then_inc(S["pre_free"], 1)
                elif u in XPROJ:
                    a(xdbl[:, XPROJ.index(u), :], bank[0:XD, :], ACT.Identity).then_inc(S["pre_free"], 1)
                elif u in DT_F + DT_B:
                    dr, c = (0, DT_F.index(u)) if u in DT_F else (1, DT_B.index(u))
                    if c == 0 and k is not None:
                        at_least(act, "rest_ready", kk, 4, 2 * dr)
                    top, e = soft_buffers(kk, dr)[:2]
                    a(top[:, c, :], bank, ACT.Relu, bias=chan[:, 1, c:c + 1])
                    a(e[:, c, :], bank, ACT.Abs, bias=chan[:, 1, c:c + 1]).then_inc(S["pre_free"], 1)
                else:
                    dr, which = (0, REP_F.index(u)) if u in REP_F else (1, REP_B.index(u))
                    if u == REP_F[0]:
                        at_least(act, "prod_ready", kk, PAIRS, -PAIRS)
                    a(rep[:, par, dr, which, :], bank, ACT.Identity).then_inc(S["pre_free"], 1)

            def silu(k, kk, par):
                at_least(act, "pre_free", *pre_use(k, GATE[-1], kk))
                a(gate[:, par, :, :], gate[:, par, :, :], ACT.Silu)
                at_least(act, "conv_ready", kk, CONVS, CONVS)
                for dr in range(2):
                    a(xc[:, par, dr, :, :], xc[:, par, dr, :, :], ACT.Silu).then_inc(S["silu_done"], 1)

            def soft_exp(k, kk, dr):
                at_least(act, "pre_free", *pre_use(k, (DT_F, DT_B)[dr][-1], kk))
                e = soft_buffers(kk, dr)[1]
                a(e, e, ACT.Exp, scale=-1.0).then_inc(S["soft_e"], 1)

            def soft_ln(kk, dr):
                at_least(act, "soft_e", kk, 2, dr + 1)
                if not (isinstance(kk, int) and kk == 0):
                    at_least(act, "lo_ready", kk, 4, 2 * dr)
                _, e, one_e, ln = soft_buffers(kk, dr)
                a(one_e, e, ACT.Identity, bias=1.0)
                a(ln, e, ACT.Ln, bias=1.0).then_inc(S["soft_l"], 1)

            def split_hi(kk, dr, i):
                at_least(act, "dt_ready", kk, 4, 2 * dr + i + 1)
                at_least(act, SENT[1 - dr][i], kk, MOVES, (dr - 1) * MOVES + dr * MOVES)
                a(parts[:, i, 0, :], soft_buffers(kk, dr)[i].rearrange("p c x -> p (c x)"), ACT.Identity)\
                    .then_inc(S["hi_ready"], 1)

            def split_mid(kk, dr, i):
                at_least(act, "rest_ready", kk, 4, 2 * dr + i + 1)
                a(parts[:, i, 1, :], soft_buffers(kk, dr)[2 + i].rearrange("p c x -> p (c x)"), ACT.Identity)\
                    .then_inc(S["mid_ready"], 1)

            def gelu(kk):
                at_least(act, "post_free", kk, POST_USES, FC2)
                a(gl4, gl4, ACT.Gelu).then_inc(S["gelu_done"], 1)

            def post(kk, u):
                if u in (NORM_T, NORM_T + 1):
                    full("post_full", kk, POST_USES, u)
                    half = u - NORM_T
                    a(pT[:, half, :], POST[0:HALF, :], ACT.Identity, scale=gains[:, 2, half:half + 1],
                      bias=gains[:, 3, half:half + 1]).then_inc(S["post_free"], 1)
                elif FC1 <= u < FC2:
                    full("post_full", kk, POST_USES, u)
                    c = u - FC1
                    a(gl4[:, c, :, :], POST.rearrange("p (b l) -> p b l", b=PER), ACT.Identity, bias=chan[:, 3, c:c + 1]).then_inc(S["post_free"], 1)
                elif u in (FFF_T, FFF_T + 1):
                    full("post_full", kk, POST_USES, u)
                    a(pT[:, u - FFF_T, :], POST[0:HALF, :], ACT.Identity).then_inc(S["post_free"], 1)
                elif u == LOGITS:
                    full("post_full", kk, POST_USES, u)
                    a(act_l[:, :, :].rearrange("p t n -> p (t n)"), POST[:, 0:TILES * NODES], ACT.Gelu)\
                        .then_inc(S["act_ready"], 1)
                elif u == COEF_T:
                    full("post_full", kk, POST_USES, u)
                    a(coefT, POST[0:NODES, :], ACT.Identity).then_inc(S["post_free"], 1)

            def decay_of(k, n):
                c, dr, j, q = unit(n)
                at_least(act, "dt_filled", k, UNITS, n + 1)
                if n % 2 == 0:
                    at_least(act, "state_ready", k, PAIRS, (n - RING_A) // 2 + 1)
                g = c * 16 + q * 4 + j
                lo = 1 if dr == 0 else 0
                src = DT[n % RING_D].rearrange("p (b l) -> p b l", b=PER)[:, :, lo:lo + L - 1]
                dst = decay[:, n % RING_A // 2, n % 2 * COLS + 1:][:, 0:COLS].rearrange("p (b l) -> p b l", b=PER)[:, :, 0:L - 1]
                a(dst, src, ACT.Exp, scale=a_log[:, dr, g:g + 1]).then_inc(S["decay_ready"], 1)

            def body(k, par, pre_, pre1_, post_):
                for n in range(UNITS):
                    decay_of(k, n)
                    u = PRE_TAKEN.get(n)
                    if u in SECOND:
                        if pre1_:
                            pre(k, k + 2, par, u)
                    elif u is not None and pre_:
                        pre(k, k + 1, 1 - par, u)
                    if pre_:
                        if n == SILU_AT:
                            silu(k, k + 1, 1 - par)
                        for dr in range(2):
                            if n == SOFT_EXP[dr]:
                                soft_exp(k, k + 1, dr)
                            if n == SOFT_LN[dr]:
                                soft_ln(k + 1, dr)
                            if n in SPLIT_HI[dr]:
                                split_hi(k + 1, dr, SPLIT_HI[dr].index(n))
                            if n in SPLIT_MID[dr]:
                                split_mid(k + 1, dr, SPLIT_MID[dr].index(n))
                    if post_ and n in POST_TAKEN:
                        post(k - 1, POST_TAKEN[n])
                    if post_ and n == GELU_AT:
                        gelu(k - 1)

            act.wait_ge(S["diag_ready"], 1)
            act.wait_ge(S["w_loaded"], 16 * len(WLOADS))
            for u, kk in PROLOGUE:
                pre(None, kk, kk % 2, u)
                if (u, kk) == (GATE[-1], 0):
                    silu(None, 0, 0)
                if (u, kk) == (DT_F[-1], 0):
                    soft_exp(None, 0, 0)
                    soft_ln(0, 0)
                if (u, kk) == (DT_B[-1], 0):
                    soft_exp(None, 0, 1)
                    for i in range(2):
                        split_hi(0, 0, i)
                if (u, kk) == (REP_F[-1], 0):
                    for i in range(2):
                        split_mid(0, 0, i)
                    soft_ln(0, 1)
                if (u, kk) == (REP_B[-1], 0):
                    split_hi(0, 1, 0)
                if (u, kk) == (XH[1], 1):
                    split_hi(0, 1, 1)
                    for i in range(2):
                        split_mid(0, 1, i)
            body(0, 0, True, True, False)
            with act.Fori(0, 2) as it:
                body(it * 2 + 1, 1, True, True, True)
                body(it * 2 + 2, 0, True, True, True)
            body(5, 1, True, True, True)
            body(6, 0, True, False, True)
            body(7, 1, False, False, True)
            for u in range(POST_USES):
                post(7, u)
                if u == FC2 - 1:
                    gelu(7)

        @block.tensor
        def _(pe):
            mm = nc.tensor.matmul

            def post_bank(kk, i):
                at_least(pe, "post_free", kk, POST_USES, i)

            def turn(bank, src, half, full):
                for t in range(TILES):
                    i = nc.tensor.transpose(cols_of(bank[0:HALF, :], t), src[:, t, half * HALF:(half + 1) * HALF],
                                            ident[:, :])
                i.then_inc(S[full], 1)

            def pre(k, kk, par, u, s):
                bank = pre_bank(k, u, kk)
                if s == 0 and k is None:
                    made = {**dict.fromkeys(XH + GATE, PRE1[1]), **dict.fromkeys(DT_F + REP_F, XPROJ[0]),
                            **dict.fromkeys(DT_B + REP_B, XPROJ[1])}.get(u)
                    at_least(pe, "pre_free", 0, PRE_USES, max(PROLOGUE.index((u, kk)) - 1,
                                                              PROLOGUE.index((made, kk)) + 1 if made else 0))
                elif s == 0:
                    b, per, n = pre_use(k, u, kk)
                    at_least(pe, "pre_free", b, per, n - 1)
                if u in PRE1:
                    at_least(pe, "x1_ready", kk, 1, 1)
                    turn(bank, nrm, PRE1.index(u), "pre_full")
                    return
                if u in XH or u in GATE:
                    e = XH.index(u) if u in XH else CH + GATE.index(u)
                    last = mm(bank, w_in[:, s, e * 128:(e + 1) * 128], x1T[:, s, :], start=(s == 0), stop=(s == 1))
                elif u in XPROJ:
                    dr = XPROJ.index(u)
                    if s == 0:
                        at_least(pe, "silu_done", kk, 2, dr + 1)
                    last = mm(bank[0:XD, :], w_x[:, s, :], xc[:, par, dr, s, :], start=(s == 0), stop=(s == CH - 1))
                elif u in DT_F + DT_B:
                    dr, c = (0, DT_F.index(u)) if u in DT_F else (1, DT_B.index(u))
                    last = mm(bank, w_dt[:, c * 128:(c + 1) * 128], xdbl[:, dr, :], start=True, stop=True)
                else:
                    dr, which = (0, REP_F.index(u)) if u in REP_F else (1, REP_B.index(u))
                    last = mm(bank, sel_rep[:, which, :], xdbl[:, dr, :], start=True, stop=True)
                if s == PRE_AT[u][1] - 1:
                    last.then_inc(S["pre_full"], 1)

            def by_token(col, width, t, terms, stride=L):
                for b in range(1 if t < PER else PER):
                    rows, at = (slice(0, 128), t * stride + LIMG) if t < PER else \
                        (slice(b * LIMG, (b + 1) * LIMG), b * stride)
                    for i, (x, w) in enumerate(terms):
                        last = mm(ps[rows, 7, col:col + width], x[:, at:at + rows.stop - rows.start], w,
                                  start=(i == 0), stop=(i == len(terms) - 1), tile_position=(0, rows.start))
                return last

            def tokens(src, w, s, t, stride=L):
                return by_token(s * DIM, DIM, t, [(src[:, c, :], w[:, c, :]) for c in range(CH)], stride)

            def post(kk, u, s):
                if u in (OUTP, OUTP + 1):
                    if s == 0:
                        at_least(pe, "y_taken", kk, CH, CH)
                        post_bank(kk, u)
                    last = tokens(yz, w_out, s, s if u == OUTP else 2)
                    if s == POST_AT[u][1] - 1:
                        last.then_inc(S["post_full"], 1)
                elif u in (NORM_T, NORM_T + 1):
                    at_least(pe, "m_ready", kk, 1, 1)
                    post_bank(kk, u)
                    turn(POST, pnrm, u - NORM_T, "post_full")
                elif FC1 <= u < FC2:
                    if s == 0:
                        post_bank(kk, u)
                    c = u - FC1
                    last = mm(POST, w_fc1[:, s, c * 128:(c + 1) * 128], pT[:, s, :], start=(s == 0), stop=(s == 1))
                    if s == 1:
                        last.then_inc(S["post_full"], 1)
                elif u in (FC2, FC2 + 1):
                    if s == 0:
                        at_least(pe, "gelu_done", kk, 1, 1)
                        post_bank(kk, u)
                    last = tokens(gl, w_fc2, s, s if u == FC2 else 2, L + MARGIN)
                    if s == POST_AT[u][1] - 1:
                        last.then_inc(S["post_full"], 1)
                elif u in (FFF_T, FFF_T + 1):
                    at_least(pe, "v_ready", kk, 1, 1)
                    post_bank(kk, u)
                    turn(POST, pnrm, u - FFF_T, "post_full")
                elif u == LOGITS:
                    post_bank(kk, u)
                    for t in range(TILES):
                        last = by_token(t * NODES, NODES, t, [(pT[:, i, :], w_fin[:, i, :]) for i in range(2)])
                    last.then_inc(S["post_full"], 1)
                elif u == COEF_T:
                    at_least(pe, "coef_ready", kk, 1, 1)
                    post_bank(kk, u)
                    for t in range(TILES):
                        last = nc.tensor.transpose(ps[0:NODES, 7, t * 128:(t + 1) * 128], tree[:, 1, t, :], ident[:, :])
                    last.then_inc(S["post_full"], 1)
                else:
                    post_bank(kk, u)
                    for o, t in enumerate((0, 1) if u == FFF_OUT else (2,)):
                        last = mm(ps[:, 7, o * DIM:(o + 1) * DIM], coefT[:, t * 128:(t + 1) * 128], w_fout[:, :],
                                  start=True, stop=True)
                    last.then_inc(S["post_full"], 1)

            def spread_of(k, n, i):
                c, dr, j, q = unit(n)
                if n in (0, 16):
                    at_least(pe, SENT[dr][i], k, MOVES, MOVES)
                if i == 0:
                    at_least(pe, "decay_ready", k, UNITS, n - RING_D + 1)
                    bank, full = DT[n % RING_D], "dt_filled"
                else:
                    at_least(pe, "bu_ready", k, UNITS, n - RING_W + 1)
                    bank, full = BU[n % RING_W], "bu_filled"
                mm(bank, sel_spread[:, j, :], spread[:, i, dr, c, q * COLS:(q + 1) * COLS],
                   start=True, stop=True).then_inc(S[full], 1)

            def reduce(k, par, quad):
                c, dr, j, _ = unit(4 * quad)
                if quad % 8 == 0:
                    at_least(pe, "y_taken", k, CH, c)
                    for d in range(2):
                        mm(Y, diag_skip[:, c, :], xc[:, par, d, c, :], start=(d == 0), stop=False)
                at_least(pe, "prod_ready", k, PAIRS, 2 * quad + 2)
                for q in range(4):
                    last = mm(ps[32 * q:32 * q + 32, 5, 0:COLS], sel_sum[:, j, :], hring[:, (4 * quad + q) % RING_H, :],
                              start=False, stop=(quad % 8 == 7), tile_position=(0, 32 * q))
                last.then_inc(S["reduced"], 1)

            def body(k, par, pre_, pre1_, post_):
                for n in range(UNITS):
                    spread_of(k, n, 1)
                    if n + SKEW < UNITS:
                        spread_of(k, n + SKEW, 0)
                    elif not (isinstance(k, int) and k == BLOCKS - 1):
                        spread_of(k + 1, n + SKEW - UNITS, 0)
                    if n % 4 == REDUCE_AT:
                        q = n // 4
                        if q >= 2:
                            reduce(k, par, q - 2)
                        elif not (isinstance(k, int) and k == 0):
                            reduce(k - 1, 1 - par, QUADS - 2 + q)
                    for u, (at, steps) in enumerate(PRE_AT):
                        if at <= n < at + steps:
                            if u in SECOND:
                                if pre1_:
                                    pre(k, k + 2, par, u, n - at)
                            elif pre_:
                                pre(k, k + 1, 1 - par, u, n - at)
                    if post_:
                        for u, (at, steps) in enumerate(POST_AT):
                            if at <= n < at + steps:
                                post(k - 1, u, n - at)

            pe.wait_ge(S["txt_loaded"], 5 * 16)
            pe.wait_ge(S["key_ready"], 1)
            for b in range(NSEQ):
                last = nc.tensor.transpose(ps[:, b // 4, b % 4 * 128:(b % 4 + 1) * 128], run[:, b * 128:(b + 1) * 128],
                                           ident[:, :])
            last.then_inc(S["keyT_ready"], 1)
            pe.wait_ge(S["img_loaded"], 4 * 16)
            for k in range(BLOCKS):
                if k >= 2:
                    pe.wait_ge(S["img_taken"], k - 1)
                for f in range(FK):
                    last = mm(ps[:, 4 + k % 2, 0:DIM], patches[:, f, k * 128:(k + 1) * 128], w_tok[:, f, :],
                              start=(f == 0), stop=(f == FK - 1))
                last.then_inc(S["img_ready"], 1)
            pe.wait_ge(S["w_loaded"], 16 * len(WLOADS))
            pe.wait_ge(S["diag_ready"], 1)
            for u, kk in PROLOGUE:
                for s in range(PRE_AT[u][1]):
                    pre(None, kk, kk % 2, u, s)
            pe.wait_ge(S["img_taken"], BLOCKS)
            pe.wait_ge(S["rows_zeroed"], 1)
            for n in range(SKEW):
                spread_of(0, n, 0)
            body(0, 0, True, True, False)
            with pe.Fori(0, 2) as it:
                body(it * 2 + 1, 1, True, True, True)
                body(it * 2 + 2, 0, True, True, True)
            body(5, 1, True, True, True)
            body(6, 0, True, False, True)
            body(7, 1, False, False, True)
            reduce(7, 1, QUADS - 2)
            reduce(7, 1, QUADS - 1)
            for u in range(POST_USES):
                for s in range(POST_AT[u][1]):
                    post(7, u, s)

        @block.vector
        def _(dve):
            v = nc.vector

            class Steps:

                def __init__(self, name, per):
                    self.name, self.per, self.n = name, per, 0

                def done(self, ins, kk):
                    self.n += 1
                    ins.then_inc(S[self.name], 1)
                    dve.wait_ge(S[self.name], kk * self.per + self.n)

            once = Steps("pro", 0)
            v.memset(decay[:, :, :], 0.0)
            v.memset(prods[:, :, :], 0.0)
            v.memset(tree[:, :, :, :], 0.0)
            dve.wait_ge(S["txt_loaded"], 5 * 16)
            once.done(v.tensor_tensor(eq, shifted.bitcast(I32), plain.bitcast(I32), ALU.is_equal), 0)
            once.done(v.memset(shifted, 1.0), 0)
            once.done(v.tensor_tensor_scan(run, shifted, eq, 0.0, ALU.add, ALU.mult), 0)
            js = jrow.rearrange("p (o i) -> p o i", o=1).broadcast_to([128, NSEQ, LTXT])
            as3 = lambda x: x.rearrange("p (b i) -> p b i", b=NSEQ)
            once.done(v.scalar_tensor_tensor(as3(shifted), as3(run), 128.0, js, ALU.mult, ALU.add), 0)
            v.tensor_tensor(run, shifted, eq, ALU.mult).then_inc(S["key_ready"], 1)
            dve.wait_ge(S["w_loaded"], 16 * len(WLOADS))
            v.tensor_scalar(a_log[:, :, :], a_log[:, :, :], 80.0, None, ALU.min).then_inc(S["exp_a"], 1)
            v.tensor_copy(sel_spread[:, :, :].rearrange("p j m -> p (j m)"), sel_raw)
            for c in range(CH):
                v.tensor_scalar(diag_skip[:, c, :], ident[:, :], chan[:, 2, c:c + 1], None, ALU.mult)
            dve.wait_ge(S["a_ready"], 1)
            v.tensor_scalar(a_log[:, :, :], a_log[:, :, :], -1.0, None, ALU.mult).then_inc(S["diag_ready"], 1)
            dve.wait_ge(S["keyT_ready"], 1)
            once.done(v.tensor_reduce(best[:, :], ps[:, 0:4, :].rearrange("p a (b j) -> p (a b) j", j=128), AX.X,
                                      ALU.max), 0)
            v.tensor_scalar(flag[:, :], best[:, :], 128.0, None, ALU.is_ge)
            once.done(v.tensor_copy(besti[:, 0, :], best[:, :]), 0)
            once.done(v.tensor_scalar(besti[:, 0, :], besti[:, 0, :], 127, None, ALU.bitwise_and), 0)
            v.tensor_tensor(besti[:, 1, :], besti[:, 0, :], boff[:, :], ALU.add).then_inc(S["rosa_idx"], 1)
            dve.wait_ge(S["img_loaded"], 4 * 16)
            once.done(v.tensor_tensor(pos, pos, tok_bias, ALU.add), 0)
            for k in range(BLOCKS):
                dve.wait_ge(S["img_ready"], k + 1)
                v.tensor_tensor(tile(k, 2), ps[:, 4 + k % 2, 0:DIM], pos, ALU.add).then_inc(S["img_taken"], 1)
            dve.wait_ge(S["img_taken"], BLOCKS)

            def mask_text(b0, b1):
                for b in range(b0, b1):
                    x = tile(b // PER, b % PER)
                    last = v.tensor_scalar(x, x, flag[:, b:b + 1], None, ALU.mult)
                last.then_inc(S["text_masked"], 1)

            PRE_V = 5

            def after(sem_name, value):
                dve.wait_ge(S[sem_name], value)
                v.memset(pad[:, :], 0.0)

            def pre1(k, kk, step):
                if step == 0:
                    for t in range(TILES):
                        last = v.bn_stats(st[:, t, :], tile(kk, t))
                    last.then_inc(S["pre_v"], 1)
                    after("pre_v", kk * PRE_V + 1)
                    for t in range(TILES):
                        last = v.bn_aggr(mv1[:, :, t], st[:, t, :])
                    last.then_inc(S["pre_v"], 1)
                    dve.wait_ge(S["pre_v"], kk * PRE_V + 2)
                    v.tensor_copy(mean0[:, bass.ds(kk * TILES, TILES)], mv1[:, 0, :]).then_inc(S["mean_kept"], 1)
                    v.tensor_scalar(ve[:, :], mv1[:, 1, :], EPS, None, ALU.add).then_inc(S["ln0_ve"], 1)
                elif step == 1:
                    at_least(dve, "ln0_rs", kk, 1, 1)
                    at_least(dve, "mean_kept", kk, 1, 1)
                    if k is not None and not (isinstance(k, int) and k == 0):
                        at_least(dve, "pre_full", *pre_use(k - 1, PRE1[1]))
                    elif kk:
                        at_least(dve, "pre_full", *pre_use(None, PRE1[1], kk - 1))
                    for t in range(TILES):
                        last = v.tensor_scalar(nrm[:, t, :], tile(kk, t), mean0[:, bass.ds(kk * TILES + t, 1)],
                                               rs0[:, bass.ds(kk * TILES + t, 1)], ALU.subtract, ALU.mult)
                    last.then_inc(S["pre_v"], 1)
                    dve.wait_ge(S["pre_v"], kk * PRE_V + 3)
                    for t in range(TILES):
                        last = v.bn_stats(st[:, t, :], nrm[:, t, :])
                    last.then_inc(S["pre_v"], 1)
                    after("pre_v", kk * PRE_V + 4)
                    for t in range(TILES):
                        last = v.bn_aggr(mv1[:, :, t], st[:, t, :])
                    last.then_inc(S["pre_v"], 1)
                    dve.wait_ge(S["pre_v"], kk * PRE_V + 5)
                    v.tensor_scalar(ve[:, :], mv1[:, 1, :], EPS, None, ALU.add).then_inc(S["ln1_ve"], 1)
                else:
                    at_least(dve, "ln1_rs", kk, 1, 1)
                    for t in range(TILES):
                        last = v.tensor_scalar(nrm[:, t, :], nrm[:, t, :], mv1[:, 0, t:t + 1], rs1[:, t:t + 1],
                                               ALU.subtract, ALU.mult)
                    last.then_inc(S["x1_ready"], 1)

            def flat(x):
                return x.rearrange("p c x -> p (c x)")

            def soft(kk, par, dr, step):
                base = kk * 4 + 2 * dr
                dt, e, one_e, ln = (flat(x) for x in soft_buffers(kk, dr))
                if step == 0:
                    at_least(dve, "soft_l", kk, 2, dr + 1)
                    v.scalar_tensor_tensor(one_e, one_e, -1.0, e, ALU.add, ALU.subtract).then_inc(S["soft_v"], 1)
                elif step == 1:
                    dve.wait_ge(S["soft_v"], base + 1)
                    v.tensor_tensor(ln, ln, one_e, ALU.subtract).then_inc(S["soft_v"], 1)
                elif step == 2:
                    dve.wait_ge(S["soft_v"], base + 2)
                    v.tensor_tensor(dt, dt, ln, ALU.add).then_inc(S["dt_ready"], 1)
                else:
                    dve.wait_ge(S["dt_ready"], base + 1)
                    v.tensor_tensor(e, dt, flat(xc[:, par, dr, :, :]), ALU.mult).then_inc(S["dt_ready"], 1)

            def rest(kk, dr, i):
                x = soft_buffers(kk, dr)
                at_least(dve, "hi_ready", kk, 4, 2 * dr + i + 1)
                v.tensor_tensor(flat(x[2 + i]), flat(x[i]), parts[:, i, 0, :], ALU.subtract)\
                    .then_inc(S["rest_ready"], 1)

            def low(kk, dr, i):
                at_least(dve, "mid_ready", kk, 4, 2 * dr + i + 1)
                v.tensor_tensor(parts[:, i, 2, :], flat(soft_buffers(kk, dr)[2 + i]), parts[:, i, 1, :], ALU.subtract)\
                    .then_inc(S["lo_ready"], 1)

            def take_y(k, par, c):
                at_least(dve, "reduced", k, QUADS, 8 * c + 8)
                if c == 0:
                    at_least(dve, "post_full", k, POST_USES, OUTP + 2 - POST_USES)
                if c == 1:
                    at_least(dve, "post_full", k, POST_USES, FFF_T + 2 - POST_USES)
                v.tensor_tensor(yz[:, c, :], Y, gate[:, par, c, :], ALU.mult).then_inc(S["y_taken"], 1)

            POST_V = 5

            def two(x, u, first):
                return x[:, 0:2, :] if u == first else x[:, 2:3, :]

            def bank(u, first):
                n = 2 if u == first else 1
                return ps[:, 7, 0:n * DIM].rearrange("p (t d) -> p t d", d=DIM)

            def post(kk, u):
                if u in (OUTP, OUTP + 1):
                    at_least(dve, "post_full", kk, POST_USES, u + 1)
                    tiles = (0, 1) if u == OUTP else (2,)
                    for t in tiles:
                        last = v.tensor_scalar(hh[:, t, :], tile(kk, t), mean0[:, bass.ds(kk * TILES + t, 1)],
                                               rs0[:, bass.ds(kk * TILES + t, 1)], ALU.subtract, ALU.mult)
                    last.then_inc(S["hh_u"], 1)
                    dve.wait_ge(S["hh_u"], kk * 2 + u + 1)
                    x = two(hh, u, OUTP)
                    v.tensor_tensor(x, bank(u, OUTP), x, ALU.add).then_inc(S["post_free"], 1)
                elif u in (FC2, FC2 + 1):
                    at_least(dve, "post_full", kk, POST_USES, u + 1)
                    at_least(dve, "out_sent", kk, 64, 0)
                    x = two(h1, u, FC2)
                    v.tensor_tensor(x, bank(u, FC2), two(hh, u, FC2), ALU.add).then_inc(S["post_free"], 1)
                    dve.wait_ge(S["post_free"], kk * POST_USES + u + 1)
                    n = 2 if u == FC2 else 1
                    t = 0 if u == FC2 else 2
                    v.tensor_tensor(x, x, h0[:, bass.ds((kk * TILES + t) * DIM, n * DIM)]
                                    .rearrange("p (t d) -> p t d", d=DIM), ALU.add).then_inc(S["h1_sum"], 1)
                elif u in (FFF_OUT, FFF_OUT + 1):
                    at_least(dve, "post_full", kk, POST_USES, u + 1)
                    x = two(h1, u, FFF_OUT)
                    v.tensor_tensor(x, bank(u, FFF_OUT), x, ALU.add).then_inc(S["post_free"], 1)

            def post_norm(kk, which, part):
                src = (hh, h1)[which]
                base = kk * 4 + 2 * which
                if part == 0:
                    if which == 0:
                        at_least(dve, "post_free", kk, POST_USES, OUTP + 2)
                    else:
                        at_least(dve, "h1_sum", kk, 2, 2)
                    for t in range(TILES):
                        last = v.bn_stats(pst[:, t, :], src[:, t, :])
                    last.then_inc(S["post_v"], 1)
                    after("post_v", base + 1)
                    for t in range(TILES):
                        last = v.bn_aggr(pmv[:, :, t], pst[:, t, :])
                    last.then_inc(S["post_v"], 1)
                    dve.wait_ge(S["post_v"], base + 2)
                    v.tensor_scalar(pve[:, :], pmv[:, 1, :], EPS, None, ALU.add)\
                        .then_inc(S[("hh_ve", "h1_ve")[which]], 1)
                else:
                    at_least(dve, ("hh_rs", "h1_rs")[which], kk, 1, 1)
                    for t in range(TILES):
                        last = v.tensor_scalar(pnrm[:, t, :], src[:, t, :], pmv[:, 0, t:t + 1], prs[:, t:t + 1],
                                               ALU.subtract, ALU.mult)
                    last.then_inc(S[("m_ready", "v_ready")[which]], 1)
                    if which == 0:
                        dve.wait_ge(S["m_ready"], kk + 1)
                        v.tensor_tensor(hh[:, :, :], hh[:, :, :], fc2_bias[:, :].rearrange("p (o d) -> p o d", o=1)
                                        .broadcast_to([128, TILES, DIM]), ALU.add).then_inc(S["hh_b"], 1)
                        dve.wait_ge(S["hh_b"], kk + 1)

            TREE_V = 11

            def walk(kk):
                s = Steps("tree_v", TREE_V)
                reached, coef = tree[:, 0, :, :], tree[:, 1, :, :]
                at_least(dve, "act_ready", kk, 1, 1)
                v.tensor_scalar(go_r[:, 0, :, :], ps[:, 7, 0:TILES * NODES].rearrange("p (t n) -> p t n", n=NODES),
                                0.0, None, ALU.is_gt).then_inc(S["post_free"], 1)
                dve.wait_ge(S["post_free"], kk * POST_USES + LOGITS + 1)
                s.done(v.tensor_scalar(go_l[:, 0, :, :], go_r[:, 0, :, :], -1.0, 1.0, ALU.mult, ALU.add), kk)
                v.tensor_tensor(go_r[:, 1, :, :], go_r[:, 0, :, :], act_l[:, :, :], ALU.mult)
                s.done(v.tensor_tensor(go_l[:, 1, :, :], go_l[:, 0, :, :], act_l[:, :, :], ALU.mult), kk)
                v.tensor_copy(tree[:, :, :, 1:2], go_l[:, :, :, 0:1])
                s.done(v.tensor_copy(tree[:, :, :, 2:3], go_r[:, :, :, 0:1]), kk)

                def level(n0, n1):
                    m = tree[:, 0:1, :, n0:n1].broadcast_to([128, 2, TILES, n1 - n0])
                    for off, go in ((1, go_l), (2, go_r)):
                        last = v.tensor_tensor(tree[:, :, :, 2 * n0 + off:2 * n1 + off - 1:2], m, go[:, :, :, n0:n1],
                                               ALU.mult)
                    s.done(last, kk)

                level(1, 3)
                level(3, 7)
                level(7, 10)
                s.done(v.tensor_reduce(tsum[:, 0, :], reached[:, :, 10:15], AX.X, ALU.add), kk)
                s.done(v.tensor_tensor(reached[:, :, 20], reached[:, :, 20], tsum[:, 0, :], ALU.add), kk)
                s.done(v.tensor_tensor(go_r[:, 0, :, 10:21], reached[:, :, 10:21], act_l[:, :, 10:21], ALU.mult), kk)
                s.done(v.tensor_reduce(tsum[:, 1, :], go_r[:, 0, :, 10:21], AX.X, ALU.add), kk)
                s.done(v.tensor_tensor(coef[:, :, 20], coef[:, :, 20], tsum[:, 1, :], ALU.add), kk)
                v.scalar_tensor_tensor(coef[:, :, 20], act_l[:, :, 20], 5.0, coef[:, :, 20], ALU.mult, ALU.add)\
                    .then_inc(S["coef_ready"], 1)
                assert s.n == TREE_V, s.n

            def times_b(k, par, n):
                c, dr, j, q = unit(n)
                at_least(dve, "bu_filled", k, UNITS, n + 1)
                if n in (0, 16):
                    u = (REP_F, REP_B)[dr][1]
                    at_least(dve, "pre_free", *(pre_use(None, u, 0) if isinstance(k, int) and k == 0 else
                                                pre_use(k - 1, u)))
                if n % 4 == 0:
                    at_least(dve, "reduced", k, QUADS, n // 4 - 2)
                v.tensor_tensor(hring[:, n % RING_H, :], BU[n % RING_W], rep[:, par, dr, 0, :], ALU.mult)\
                    .then_inc(S["bu_ready"], 1)

            def scan(k, pair):
                n = 2 * pair
                c, dr, j, q = unit(n)
                at_least(dve, "decay_ready", k, UNITS, n + 2)
                at_least(dve, "bu_ready", k, UNITS, n + 2)
                way = slice(None, None, 1 if dr == 0 else -1)
                h = hring[:, n % RING_H:n % RING_H + 2, :].rearrange("p a b -> p (a b)")[:, way]
                v.tensor_tensor_scan(h, decay[:, n % RING_A // 2, dr:dr + 2 * COLS][:, way], h, 0.0, ALU.mult,
                                     ALU.add).then_inc(S["state_ready"], 1)

            def body(k, par, pre, pre1_, post_):
                for n in range(UNITS):
                    times_b(k, par, n)
                    if n % 2 and n > 1:
                        scan(k, n // 2 - 1)
                    elif n == 1 and not (isinstance(k, int) and k == 0):
                        scan(k - 1, PAIRS - 1)
                    if n in TAKE_AT:
                        c = TAKE_AT[n]
                        if c < CH - 1:
                            take_y(k, par, c)
                        elif not (isinstance(k, int) and k == 0):
                            take_y(k - 1, 1 - par, c)
                    if pre:
                        for dr in range(2):
                            if n in SOFT_V[dr]:
                                soft(k + 1, 1 - par, dr, SOFT_V[dr].index(n))
                            if n in SPLIT_REST[dr]:
                                rest(k + 1, dr, SPLIT_REST[dr].index(n))
                            if n in SPLIT_LO[dr]:
                                low(k + 1, dr, SPLIT_LO[dr].index(n))
                    if pre1_ and n in LN_AT:
                        pre1(k, k + 2, LN_AT.index(n))
                    if post_:
                        if n in POST_TAKEN:
                            post(k - 1, POST_TAKEN[n])
                        for which, at in enumerate((NORM0_AT, NORM1_AT)):
                            if n in at:
                                post_norm(k - 1, which, at.index(n))
                        if n == WALK_AT:
                            walk(k - 1)

            dve.wait_ge(S["emb_lo"], 16 * FIRST)
            mask_text(0, FIRST)
            dve.wait_ge(S["text_masked"], 1)
            for kk in range(2):
                for step in range(3):
                    pre1(None, kk, step)
            for i in range(CONVS):
                conv(v, None, 0, 0, i)
            for dr in range(2):
                for step in range(4):
                    soft(0, 0, dr, step)
                for i in range(2):
                    rest(0, dr, i)
                for i in range(2):
                    low(0, dr, i)
            dve.wait_ge(S["emb_hi"], 16 * (NSEQ - FIRST))
            mask_text(FIRST, NSEQ)
            dve.wait_ge(S["text_masked"], 2)
            dve.wait_ge(S["lo_ready"], 4)
            body(0, 0, True, True, False)
            with dve.Fori(0, 2) as it:
                body(it * 2 + 1, 1, True, True, True)
                body(it * 2 + 2, 0, True, True, True)
            body(5, 1, True, True, True)
            body(6, 0, True, False, True)
            body(7, 1, False, False, True)
            scan(7, PAIRS - 1)
            take_y(7, 1, CH - 1)
            post(7, OUTP)
            post(7, OUTP + 1)
            post_norm(7, 0, 0)
            post_norm(7, 0, 1)
            post(7, FC2)
            post(7, FC2 + 1)
            post_norm(7, 1, 0)
            post_norm(7, 1, 1)
            walk(7)
            post(7, FFF_OUT)
            post(7, FFF_OUT + 1)


def constants():
    import numpy as np

    spread = np.zeros((4, 32, 4, STATE, 8), np.float32)
    total = np.zeros((STATE, 8, 4, 32), np.float32)
    for j in range(4):
        for d in range(8):
            spread[0:3, 8 * j + d, j, :, d] = 1
            total[:, d, j, 8 * j + d] = 1
    rep = np.zeros((XD, 2, STATE, 8), np.float32)
    for n in range(STATE):
        rep[n, 0, n, :] = 1
        rep[STATE + n, 1, n, :] = 1
    pos = np.arange(LTXT)
    return {
        "c_spread": spread.reshape(128, 4 * 128), "c_sum": total.reshape(128, 4, 32),
        "c_rep": rep.reshape(XD, 2, 128), "c_ident": np.eye(128, dtype=np.float32),
        "c_jrow": (pos[:, None] + pos[None, :] - 128).astype(np.float32),
        "c_boff": np.tile(np.arange(NSEQ) * LTXT + 1, (128, 1)).astype(np.int32),
    }


def kernel(x, x_txt, L0_tok_proj_w, L0_tok_proj_b, L0_tok_pos_emb, L0_txt_emb, L0_attn_g1, L0_attn_b1,
           L0_attn_in_proj_w, L0_attn_conv_w, L0_attn_conv_b, L0_attn_x_proj_w, L0_attn_dt_proj_w, L0_attn_dt_proj_b,
           L0_attn_A_log, L0_attn_A_b_log, L0_attn_Dskip, L0_attn_out_proj_w, L0_attn_g2, L0_attn_b2, L0_attn_fc1_w,
           L0_attn_fc1_b, L0_attn_fc2_w, L0_attn_fc2_b, L0_ffn_weights_in, L0_ffn_weights_out):
    import concourse.bacc as bacc
    import numpy as np
    from concourse.bass_utils import run_bass_kernel_spmd

    def chunks(w, n):
        w = np.asarray(w)
        return w.reshape(n, w.shape[0] // n, *w.shape[1:]).swapaxes(0, 1)

    side = 128 // PATCH
    px = np.asarray(x).reshape(NSEQ, 2, side, PATCH, side, PATCH).transpose(0, 1, 2, 4, 3, 5)
    px = px.reshape(NSEQ * LIMG, FEAT).T
    ids = np.asarray(x_txt)
    xw = np.asarray(L0_attn_x_proj_w)
    xw = np.concatenate([xw[RANK:], xw[:RANK]])
    dtw = np.zeros((XD, INNER), np.float32)
    dtw[2 * STATE:] = np.asarray(L0_attn_dt_proj_w).T
    spread_a = lambda a: np.asarray(a).reshape(48, 8, STATE).transpose(2, 1, 0).reshape(128, 48)
    arrays = {
        "patches": chunks(px, FK), "w_tok": chunks(np.asarray(L0_tok_proj_w).T, FK),
        "pos": np.tile(np.asarray(L0_tok_pos_emb)[0], (PER, 1)),
        "tok_bias": np.tile(np.asarray(L0_tok_proj_b), (128, 1)),
        "x_pad": np.concatenate([np.full_like(ids, -1), ids], 1), "x_ids": ids.reshape(-1, 1),
        "emb": np.asarray(L0_txt_emb),
        "w_in": chunks(np.asarray(L0_attn_in_proj_w).T, 2), "w_x": chunks(xw.T, CH), "w_dt": dtw,
        "w_out": chunks(np.asarray(L0_attn_out_proj_w).T, CH), "w_fc1": chunks(np.asarray(L0_attn_fc1_w).T, 2),
        "w_fc2": chunks(np.asarray(L0_attn_fc2_w).T, CH), "w_fin": chunks(np.asarray(L0_ffn_weights_in).T, 2),
        "w_fout": np.asarray(L0_ffn_weights_out), "taps": chunks(L0_attn_conv_w, CH),
        "chan": np.stack([chunks(a, CH) for a in (L0_attn_conv_b, L0_attn_dt_proj_b, L0_attn_Dskip, L0_attn_fc1_b)], 1),
        "gains": np.stack([chunks(a, 2) for a in (L0_attn_g1, L0_attn_b1, L0_attn_g2, L0_attn_b2)], 1),
        "fc2_bias": np.tile(np.asarray(L0_attn_fc2_b), (128, 1)),
        "a_log": np.stack([spread_a(L0_attn_A_log), spread_a(L0_attn_A_b_log)], 1),
        **constants(),
    }
    nc = bacc.Bacc("TRN2", target_bir_lowering=False, num_devices=1)
    given, aps = {}, {}
    for name, a in arrays.items():
        given[f"in_{name}"] = a = np.ascontiguousarray(a)
        aps[name] = nc.dram_tensor(f"in_{name}", a.shape, mybir.dt.from_np(a.dtype), kind="ExternalInput").ap()
    out = nc.dram_tensor("out_0", (NSEQ, L, DIM), F32, kind="ExternalOutput").ap()
    build(nc, aps, out)
    r = run_bass_kernel_spmd(nc, [given], core_ids=[0])
    return r.results[0]["out_0"]
```
